# Optimizing a Trainium2 kernel written in Bass

```python
import numpy as np
import jax
import jax.numpy as jnp

def _softmax(x, axis=-1):
    return jax.nn.softmax(x, axis=axis)

def _gelu(x):
    return jax.nn.gelu(x, approximate=True)

def _silu(x):
    return jax.nn.silu(x)

def _sigmoid(x):
    return jax.nn.sigmoid(x)

def _layernorm(x, axis=-1, eps=1e-05):
    m = jnp.mean(x, axis=axis, keepdims=True)
    v = jnp.var(x, axis=axis, keepdims=True)
    return (x - m) / jnp.sqrt(v + eps)

def _scatter_add(tgt, idx, src, axis=0):
    return tgt.at[idx].add(src)

def _segment_sum(src, seg, n):
    return jax.ops.segment_sum(src, seg, n)
kernel_name = 'mk_gnn_preln_d2_gnn_r8_7c22e3'

def setup_inputs(seed: int=0):
    np.random.seed(seed)
    _w = jnp.asarray

    def _rec_inputs():
        import jax
        import jax.numpy as jnp
        _gk = jax.random.key(seed)
        x = -6.415e-05 + 1 * jax.random.normal(jax.random.fold_in(_gk, 1), (6250, 512), jnp.float32)
        _s = jax.random.randint(jax.random.fold_in(_gk, 2), (50000,), 0, 6250, jnp.int32)
        _d = jax.random.randint(jax.random.fold_in(_gk, 3), (50000,), 0, 6250, jnp.int32)
        _loop = jnp.arange(6250, dtype=jnp.int32)
        src = jnp.concatenate([_s, _d, _loop])
        dst = jnp.concatenate([_d, _s, _loop])
        _o = jnp.argsort(dst, stable=True)
        src = src[_o]
        dst = dst[_o]
        edge_weight = jax.random.uniform(jax.random.fold_in(_gk, 13), (106250,), jnp.float32, 0.0, 0.999994)
        return (x, src, dst, edge_weight)
    x, src, dst, edge_weight = _rec_inputs()

    def _L0_gnn_setup():
        import jax, jax.numpy as jnp
        import numpy as np
        N_NODES = 2500
        N_EDGES = 20000
        N_IN = 512
        N_OUT = 512
        key = jax.random.key(seed)
        k1, k2, k3, k4, k5 = jax.random.split(key, 5)
        x = jax.random.normal(k1, (N_NODES, N_IN), dtype=jnp.float32)
        vals = jax.random.uniform(k2, (N_EDGES,), dtype=jnp.float32)
        bound = 1.0 / np.sqrt(N_IN)
        weight = jax.random.uniform(k3, (N_OUT, N_IN), minval=-bound, maxval=bound, dtype=jnp.float32)
        row = jax.random.randint(k4, (N_EDGES,), 0, N_NODES, dtype=jnp.int32)
        col = jax.random.randint(k5, (N_EDGES,), 0, N_NODES, dtype=jnp.int32)
        return {'x': x, 'vals': vals, 'weight': weight, 'row': row, 'col': col}
    _L0_gnn_all = _L0_gnn_setup()
    _L0_gnn_in = {k: v for k, v in _L0_gnn_all.items() if k in ('weight',)}
    del _L0_gnn_all

    def _L1_gnn_setup():
        import jax, jax.numpy as jnp
        import numpy as np
        N_NODES = 6250
        D_IN = 512
        D_OUT = 512
        N_EDGES = 50000
        key = jax.random.key(seed)
        k1, k2, k3, k4 = jax.random.split(key, 4)
        features = jax.random.normal(k1, (N_NODES, D_IN), dtype=jnp.float32)
        limit = float(np.sqrt(6.0 / (D_IN + D_OUT)))
        weight = jax.random.uniform(k2, (D_IN, D_OUT), dtype=jnp.float32, minval=-limit, maxval=limit)
        edge_index = jax.random.randint(k3, (2, N_EDGES), 0, N_NODES, dtype=jnp.int64)
        edge_vals = jax.random.uniform(k4, (N_EDGES,), dtype=jnp.float32)
        return {'features': features, 'weight': weight, 'edge_vals': edge_vals, 'edge_index': edge_index}
    _L1_gnn_all = _L1_gnn_setup()
    _L1_gnn_in = {k: v for k, v in _L1_gnn_all.items() if k in ('weight',)}
    del _L1_gnn_all
    return {'x': x, 'src': src, 'dst': dst, 'edge_weight': edge_weight, 'L0_gnn_weight': _L0_gnn_in['weight'], 'L1_gnn_weight': _L1_gnn_in['weight']}

def reference(x, src, dst, edge_weight, L0_gnn_weight, L1_gnn_weight):
    import jax
    import jax.numpy as jnp

    def _L0_gnn_ref(x, vals, weight, row, col):
        import jax, jax.numpy as jnp
        import numpy as np
        N_NODES = 2500
        N_EDGES = 20000
        N_IN = 512
        N_OUT = 512
        n = x.shape[0]
        msgs = x[col] * vals[:, None]
        agg = jax.ops.segment_sum(msgs, row, num_segments=n)
        return jnp.einsum('nd,od->no', agg, weight)

    def _L1_gnn_ref(features, weight, edge_vals, edge_index):
        import jax, jax.numpy as jnp
        import numpy as np
        N_NODES = 6250
        D_IN = 512
        D_OUT = 512
        N_EDGES = 50000
        support = features @ weight
        row, col = (edge_index[0], edge_index[1])
        msgs = support[col] * edge_vals[:, None]
        output = jax.ops.segment_sum(msgs, row, num_segments=features.shape[0])
        return jax.nn.relu(output)
    edge_index = jnp.stack([src, dst])
    h = jnp.maximum(_layernorm(x, axis=-1), 0.0)
    x = x + _L0_gnn_ref(h, edge_weight, L0_gnn_weight, src, dst)
    h = jnp.maximum(_layernorm(x, axis=-1), 0.0)
    x = x + _L1_gnn_ref(h, L1_gnn_weight, edge_weight, edge_index)
    return x

_drawn_inputs = setup_inputs


def setup_inputs(seed=0):
    import zlib

    import numpy as np

    out = dict(_drawn_inputs(seed))
    spreads = {}
    factors = {}
    for name, (base, spread) in spreads.items():
        noise = np.random.default_rng([zlib.crc32(name.encode()), seed]).standard_normal(out[name].shape)
        drawn = base * np.exp(spread * noise) if base else spread * noise
        out[name] = jnp.asarray(drawn.astype(out[name].dtype))
    for name, factor in factors.items():
        out[name] = (out[name] * factor).astype(out[name].dtype)
    return out
```

```python
from contextlib import ExitStack

import concourse.bass as bass
from concourse import mybir
from concourse.alu_op_type import AluOpType as ALU

F32 = mybir.dt.float32
F16 = mybir.dt.float16
I32 = mybir.dt.int32
ACT = mybir.ActivationFunctionType
AX = mybir.AxisListType
DVE = mybir.EngineType.DVE

P = 128
NODES = 6250
D = 512
KB = D // P
EDGES = 106250
EPS = 1e-5

TILES = -(-NODES // P)
LAST = NODES - (TILES - 1) * P
EP = 125
EC = EDGES // EP
BC = 50
BLOCKS = EC // BC
GC = 10
GROUPS = BC // GC
UNIT = 8
REC = 2
UCOLS = -(-(-(-(EP * BC) // UNIT) + TILES) // P)
C56 = UCOLS * UNIT
BLOCK_UNITS = UCOLS * P
CHUNK_UNITS = P // UNIT
MAX_UNITS = EDGES // UNIT + BLOCKS * TILES
U = 12
H = U // 2
CHUNKS = -(-((MAX_UNITS + TILES * (CHUNK_UNITS - 1)) // CHUNK_UNITS) // U) * U
PASSES = CHUNKS // U
TCHUNKS = -(-CHUNKS // P) * P
SPILL = CHUNKS * CHUNK_UNITS
OH = BC * TILES
ZW = OH // 2
ZR = 5
UROW = UNIT * REC
TABLE_ROWS = 4 * ZW * P // UROW
TW = TILES + 1
assert EP * EC == EDGES and BLOCKS * BC == EC and GROUPS * GC == BC
assert OH % 2 == 0 and ZW % ZR == 0 and SPILL + BLOCKS * BLOCK_UNITS <= TABLE_ROWS
assert EP * BC + TILES * (UNIT - 1) <= BLOCK_UNITS * UNIT and TCHUNKS * CHUNK_UNITS <= TABLE_ROWS


def build_gnn(nc, x, src, dst, edge_weight, w0, w1, out):
    with ExitStack() as ctx:
        def sb(name, shape, dt):
            return ctx.enter_context(nc.sbuf_tensor(name, shape, dt))

        def bcast(ap, axis, n):
            shape = list(ap.shape)
            shape.insert(axis, n)
            return ap.unsqueeze(axis).to_broadcast(shape)

        def sem(name):
            return ctx.enter_context(nc.semaphore(name))

        table = nc.dram_tensor("sorted_units", [TABLE_ROWS, UROW], F32).ap()
        support = [nc.dram_tensor(f"support{n}", [NODES, D], F32).ap() for n in range(2)]
        x1_dram = nc.dram_tensor("x1", [NODES, D], F32).ap()
        chunk_tile_dram = nc.dram_tensor("chunk_tile", [1, TCHUNKS], I32).ap()

        acc = sb("acc", [P, TILES * D], F32)
        onehot = acc[0:EP, 0:BLOCKS * OH // 2].bitcast(F16)
        row_ring = sb("row_ring", [P, U * D], F32)
        rows = [row_ring[:, j * D:(j + 1) * D] for j in range(U)]
        carved = [0]

        def carve(partitions, shape, dt):
            size = 1
            for n in shape:
                size *= n
            at, carved[0] = carved[0], carved[0] + size
            assert carved[0] <= U * D
            ap = row_ring[0:partitions, at:at + size]
            if dt != F32:
                ap = ap.bitcast(dt)
            if len(shape) == 2:
                ap = ap.rearrange("p (a b) -> p a b", a=shape[0])
            if len(shape) == 3:
                ap = ap.rearrange("p (a b c) -> p a b c", a=shape[0], b=shape[1])
            return ap

        work = sb("work", [P, max(BLOCKS * UCOLS * TILES, 2 * GC * (P + C56 + REC * C56))], F32)
        unit_mask = work[:, 0:BLOCKS * UCOLS * TILES]
        sel = work[:, 0:U * P].rearrange("p (j m) -> p j m", j=U)
        perm_row = [work[0:EP, h * GC * P:(h + 1) * GC * P].rearrange("p (k m) -> p k m", k=GC)
                    for h in range(2)]
        perm_col = [work[0:EP, 2 * GC * P + h * GC * C56:2 * GC * P + (h + 1) * GC * C56]
                    .rearrange("p (k m) -> p k m", k=GC) for h in range(2)]
        perm_val = [work[0:EP, 2 * GC * (P + C56) + h * GC * REC * C56:2 * GC * (P + C56) + (h + 1) * GC * REC * C56]
                    .rearrange("p (k v m) -> p k v m", k=GC, v=REC) for h in range(2)]
        row_index = sb("row_index", [P, TCHUNKS], I32)
        local_row = sb("local_row", [P, TCHUNKS], F32)
        weight = sb("weight", [P, TCHUNKS], F32)
        chunk_tile = sb("chunk_tile_sb", [1, TCHUNKS], I32)
        staged_index = sb("staged_index", [P, U], I32)
        wt = [sb(f"wt{n}", [P, KB, D], F32) for n in range(2)]
        xin = [sb(f"xin{j}", [P, D], F32) for j in range(4)]
        hid = [sb(f"hid{j}", [P, D], F32) for j in range(2)]
        hidt = [sb(f"hidt{j}", [P, D], F32) for j in range(2)]
        sup = [sb(f"sup{j}", [P, D], F32) for j in range(2)]
        stats = sb("stats", [P, 4, 6], F32)
        mv = sb("mv", [P, 4, 2], F32)
        std = sb("std", [P, 4, 1], F32)
        rstd = sb("rstd", [P, 4, 1], F32)
        nmr = sb("nmr", [P, 4, 1], F32)

        edge_src = carve(EP, [EC], I32)
        edge_dst = carve(EP, [EC], I32)
        edge_w = carve(EP, [EC], F32)
        edge_loc = carve(EP, [EC], I32)
        edge_tile = edge_loc.bitcast(F32)
        edge_pack = edge_src.bitcast(F32)
        place = sb("place", [EP, BC], F32)
        place_i = sb("place_i", [EP, BC], I32)
        prow_i = sb("prow_i", [EP, BC], I32)
        pcol_i = sb("pcol_i", [EP, BC], I32)
        prow = [sb(f"prow{h}", [EP, BC], F32) for h in range(2)]
        pcol = [sb(f"pcol{h}", [EP, BC], F32) for h in range(2)]
        ranked = [carve(EP, [GC, TILES], F32) for h in range(2)]
        col_count = sb("col_count", [P, BLOCKS, TW], F16)
        units_i = sb("units_i", [TILES, BLOCKS], I32)
        units_f = sb("units_f", [TILES, BLOCKS], F32)
        units_to = sb("units_to", [TILES, BLOCKS], F32)
        units_before = sb("units_before", [TILES, BLOCKS], F32)
        chunks_i = sb("chunks_i", [TILES, 1], I32)
        chunks_f = sb("chunks_f", [TILES, 1], F32)
        unit_start = weight[:, 0:BLOCKS * TW].rearrange("p (b t) -> p b t", b=BLOCKS)
        unit_shift = local_row[:, 0:BLOCKS * TW].rearrange("p (b t) -> p b t", b=BLOCKS)
        shift_step = carve(P, [BLOCKS, TILES], F32)
        unit_dest = sb("unit_dest", [P, BLOCKS, UCOLS], F32)
        unit_dest_i = sb("unit_dest_i", [P, BLOCKS * UCOLS], I32)
        chunk_mask = carve(P, [TCHUNKS // P, TILES], F32)
        chunk_start = sb("chunk_start", [P, TILES], F32)
        chunk_tile_f = sb("chunk_tile_f", [P, TCHUNKS // P], F32)
        chunk_tile_i = sb("chunk_tile_i", [P, TCHUNKS // P], I32)
        unit_out = [sb(f"unit_out{h}", [P, UCOLS * UNIT, REC], F32) for h in range(2)]
        dest_now = [sb(f"dest_now{h}", [P, UCOLS], I32) for h in range(2)]
        chunk_rows = [rows[g][:, 0:P * REC] for g in range(TCHUNKS // P)]
        pack_i = xin[0][:].bitcast(I32)
        loc_i = xin[1][:].bitcast(I32)
        wload = [[hid[0], hid[1], hidt[0], hidt[1]][q] for q in range(KB)]

        iota = sb("iota", [P, P], F32)
        unit_id = sb("unit_id", [P, UCOLS], F32)
        chunk_id = sb("chunk_id", [P, TCHUNKS // P], F32)
        spill = sb("spill", [P, BLOCKS], F32)
        before = sb("before", [EP, EP], F16)
        pick = sb("pick", [EP, 2 * P - 1], F16)
        col_before = sb("col_before", [P, BC], F16)
        ones16 = sb("ones16", [P, 1], F16)
        tile_before = sb("tile_before", [TILES, TW], F32)
        tile_after_neg = sb("tile_after_neg", [TILES, TW], F32)
        tile_chunks = sb("tile_chunks", [TILES, TW], F32)
        tile_same = sb("tile_same", [TILES, TW], F32)
        ident = sb("ident", [P, P], F32)
        zeros = sb("zeros", [P, ZW // ZR], F32)
        zeros_wide = bcast(zeros[:], 1, ZR)
        eps = sb("eps", [P, 1], F32)

        bank = [ctx.enter_context(nc.psum_tensor(f"bank{i}", [P, D], F32)) for i in range(8)]

        block = ctx.enter_context(nc.Block())

        filled = sem("filled")
        constants = sem("constants")
        edges_loaded = sem("edges_loaded")
        weights_loaded = sem("weights_loaded")
        table_zeroed = sem("table_zeroed")
        prep = sem("prep")
        onehot_ready = sem("onehot_ready")
        counted = sem("counted")
        col_count_ready = sem("col_count_ready")
        tile_counts = sem("tile_counts")
        unit_steps = sem("unit_steps")
        starts_ready = sem("starts_ready")
        starts_copied = sem("starts_copied")
        dest_steps = sem("dest_steps")
        chunk_tile_out = sem("chunk_tile_out")
        chunk_tile_in = sem("chunk_tile_in")
        w0t_ready = sem("w0t_ready")
        w0_copied = sem("w0_copied")
        rank_ready = sem("rank_ready")
        ranked_done = sem("ranked_done")
        placed = sem("placed")
        place_steps = sem("place_steps")
        perm_steps = sem("perm_steps")
        perm_ready = sem("perm_ready")
        permuted = sem("permuted")
        units_out = sem("units_out")
        scattered = [sem(f"scattered{h}") for h in range(2)]
        onehot_zeroed = sem("onehot_zeroed")
        rows_loaded = sem("rows_loaded")
        rows_turned = sem("rows_turned")
        table_steps = sem("table_steps")
        table_ready = sem("table_ready")

        class Dense:

            def __init__(self, n):
                self.n = n
                self.x_loaded = [sem(f"x_loaded{n}{j}") for j in range(4)]
                self.x1_ready = sem(f"x1_ready{n}")
                self.x1_stored = [sem(f"x1_stored{n}{j}") for j in range(4)]
                self.stats_done = sem(f"stats_done{n}")
                self.mv_ready = sem(f"mv_ready{n}")
                self.std_ready = sem(f"std_ready{n}")
                self.rstd_ready = sem(f"rstd_ready{n}")
                self.norm_ready = sem(f"norm_ready{n}")
                self.hid_ready = sem(f"hid_ready{n}")
                self.turned = sem(f"turned{n}")
                self.hidt_ready = sem(f"hidt_ready{n}")
                self.product = sem(f"product{n}")
                self.sup_ready = sem(f"sup_ready{n}")
                self.sup_stored = [sem(f"sup_stored{n}{j}") for j in range(2)]

        class Layer:

            def __init__(self, n):
                self.n = n
                self.index_staged = sem(f"index_staged{n}")
                self.gathered = [sem(f"gathered{n}_{j}") for j in range(U)]
                self.sel_ready = sem(f"sel_ready{n}")
                self.summed = sem(f"summed{n}")
                self.added = sem(f"added{n}")

        dense = [Dense(0), Dense(1)]
        layer = [Layer(0), Layer(1)]
        acc_zeroed = sem("acc_zeroed")
        fin_loaded = [sem(f"fin_loaded{j}") for j in range(4)]
        fin_ready = sem("fin_ready")
        fin_stored = [sem(f"fin_stored{j}") for j in range(4)]

        FILLS = 12
        CONSTANTS = 14

        def wait_alone(eng, signal, value):
            if isinstance(value, int):
                eng.wait_ge(signal, value)
            else:
                value = eng.to_reg(value)
                eng.wait_ge(filled, FILLS)
                eng.wait_ge(signal, value)

        def tiles_of(body):
            def run(eng):
                for t in range(4):
                    body(t, t, P)
                with eng.Fori(1, TILES // 4) as it:
                    for j in range(4):
                        body(it * 4 + j, j, P)
                body(TILES - 1, 0, LAST)
            return run

        def tile_rows(dram, t, n):
            if isinstance(t, int):
                return dram[t * P:t * P + n, :]
            return dram[bass.ds(t * P, n), :]

        def tile_acc(t, n):
            if isinstance(t, int):
                return acc[0:n, t * D:(t + 1) * D]
            return acc[0:n, bass.ds(t * D, D)]

        @block.sync
        def _(sp):
            for buf, dram in ((edge_src, src), (edge_dst, dst), (edge_w, edge_weight)):
                sp.dma_start(buf[:], dram.rearrange("(p c) -> p c", p=EP)).then_inc(edges_loaded, 16)
            for q in range(KB):
                sp.dma_start(wload[q][:], w0[q * P:(q + 1) * P, :]).then_inc(weights_loaded, 16)
            sp.dma_start(wt[1][:], w1.rearrange("(q p) o -> p q o", p=P)).then_inc(weights_loaded, 16)
            sp.wait_ge(filled, FILLS)
            flat = table.rearrange("r c -> (r c)").rearrange("(q p w) -> q p w", q=4, p=P)
            for q in range(4):
                sp.dma_start(flat[q].rearrange("p (z w) -> p z w", z=ZR), zeros_wide).then_inc(table_zeroed, 16)

            def load_tiles(d, source):
                def load(t, j, n):
                    if not isinstance(t, int) or t >= 4:
                        wait_alone(sp, d.hid_ready, t - 3)
                        if d.n == 1:
                            wait_alone(sp, d.x1_stored[j], (t - j) * 4)
                    sp.dma_start(xin[j][0:n, :], tile_rows(source, t, n)).then_inc(d.x_loaded[j], 16)
                return load

            def store_x1(t, j, n):
                d = dense[1]
                wait_alone(sp, d.x1_ready, t + 1)
                sp.dma_start(tile_rows(x1_dram, t, n), xin[j][0:n, :]).then_inc(d.x1_stored[j], 16)

            tiles_of(load_tiles(dense[0], x))(sp)

            sp.wait_ge(dest_steps, 9)
            sp.dma_start(chunk_tile_dram.rearrange("a (p j) -> (a p) j", p=P), chunk_tile_i[:])\
                .then_inc(chunk_tile_out, 16)
            sp.wait_ge(chunk_tile_out, 16)
            sp.dma_start(chunk_tile[:], chunk_tile_dram).then_inc(chunk_tile_in, 16)

            sp.wait_ge(scattered[0], 16 * UCOLS * -(-BLOCKS // 2))
            sp.wait_ge(scattered[1], 16 * UCOLS * (BLOCKS // 2))
            by_chunk = table[0:TCHUNKS * CHUNK_UNITS, :].rearrange("(c u) r -> c (u r)", u=CHUNK_UNITS)
            for g in range(TCHUNKS // P):
                sp.dma_start(chunk_rows[g], by_chunk[g * P:(g + 1) * P, :]).then_inc(rows_loaded, 16)

            sp.wait_ge(table_ready, 6)
            load = load_tiles(dense[1], x)

            def load_and_store(t, j, n):
                load(t, j, n)
                store_x1(t, j, n)
            load(0, 0, P)
            load(1, 1, P)

            def step(t, j):
                load(t + 2, (j + 2) % 4, P)
                store_x1(t, j, P)
            for t in range(4):
                step(t, t)
            with sp.Fori(1, TILES // 4 - 1) as it:
                for j in range(4):
                    step(it * 4 + j, j)
            for t in range(TILES - 5, TILES - 3):
                step(t, t % 4)
            load(TILES - 1, 0, LAST)
            for t in range(TILES - 3, TILES - 1):
                store_x1(t, t % 4, P)
            store_x1(TILES - 1, 0, LAST)

            sp.wait_ge(dense[1].hid_ready, TILES)
            for j in range(4):
                sp.wait_ge(dense[1].x1_stored[j], 16 * ((TILES - 1 - j) // 4 + 1))

            def load_x1(t, j, n):
                if not isinstance(t, int) or t >= 4:
                    wait_alone(sp, fin_stored[j], (t - j) * 4)
                sp.dma_start(xin[j][0:n, :], tile_rows(x1_dram, t, n)).then_inc(fin_loaded[j], 16)
            tiles_of(load_x1)(sp)

        @block.gpsimd
        def _(pool):
            g = nc.gpsimd
            for buf, value in ((before, 1.0), (pick, 0.0), (col_before, 1.0), (ones16, 1.0), (tile_before, 1.0),
                               (tile_after_neg, -1.0), (tile_chunks, float(CHUNK_UNITS)), (tile_same, 0.0),
                               (ident, 0.0), (zeros, 0.0), (eps, EPS)):
                g.memset(buf[:], value).then_inc(filled, 1)
            g.iota(unit_id[:], pattern=[[P, UCOLS]], base=0, channel_multiplier=1,
                   allow_small_or_imprecise_dtypes=True).then_inc(filled, 1)
            g.iota(iota[:], pattern=[[1, P]], base=0, channel_multiplier=0,
                   allow_small_or_imprecise_dtypes=True).then_inc(constants, 1)
            g.iota(chunk_id[:], pattern=[[1, TCHUNKS // P]], base=0, channel_multiplier=TCHUNKS // P,
                   allow_small_or_imprecise_dtypes=True).then_inc(constants, 1)
            g.iota(spill[:], pattern=[[BLOCK_UNITS, BLOCKS]], base=SPILL, channel_multiplier=0,
                   allow_small_or_imprecise_dtypes=True).then_inc(constants, 1)
            pool.wait_ge(filled, FILLS)
            for buf in (before, tile_before, tile_after_neg, tile_chunks, col_before):
                g.affine_select(out=buf[:], in_=buf[:], compare_op=ALU.is_ge, fill=0.0, base=-1,
                                pattern=[[1, buf.shape[1]]], channel_multiplier=-1).then_inc(constants, 1)
            for buf in (tile_same, ident):
                g.affine_select(out=buf[:], in_=buf[:], compare_op=ALU.not_equal, fill=1.0, base=0,
                                pattern=[[1, buf.shape[1]]], channel_multiplier=-1).then_inc(constants, 1)
            g.affine_select(out=pick[:], in_=pick[:], compare_op=ALU.not_equal, fill=1.0, base=-(P - 1),
                            pattern=[[1, 2 * P - 1]], channel_multiplier=0).then_inc(constants, 1)
            pool.wait_ge(constants, 11)
            g.memset(col_before[64:65, :], float(UNIT)).then_inc(constants, 1)
            g.memset(tile_after_neg[:, TILES:TW], 0.0).then_inc(constants, 1)
            g.memset(tile_chunks[:, TILES:TW], 0.0).then_inc(constants, 1)
            pool.wait_ge(constants, CONSTANTS)

            def scatter(b, h):
                wait_alone(pool, units_out, b * 2 + 2)
                for u in range(UCOLS):
                    g.indirect_dma_start(
                        table, bass.IndirectOffsetOnAxis(ap=dest_now[h][:, u:u + 1], axis=0),
                        unit_out[h][:, u * UNIT:(u + 1) * UNIT, :].rearrange("p r v -> p (r v)"), None).then_inc(scattered[h], 16)

            def zero_onehot(b):
                wait_alone(pool, ranked_done, b * GROUPS + GROUPS)
                if isinstance(b, int):
                    g.tensor_copy(acc[:, b * ZW:(b + 1) * ZW].rearrange("p (z w) -> p z w", z=ZR), zeros_wide).then_inc(onehot_zeroed, 1)
                else:
                    g.tensor_copy(acc[:, bass.ds(b * ZW, ZW)].rearrange("p (z w) -> p z w", z=ZR), zeros_wide).then_inc(onehot_zeroed, 1)

            pool.wait_ge(table_zeroed, 64)
            g.memset(acc[:, BLOCKS * ZW:TILES * D], 0.0).then_inc(onehot_zeroed, 1)
            with pool.Fori(0, BLOCKS // 2) as it:
                for h in range(2):
                    zero_onehot(it * 2 + h)
                    scatter(it * 2 + h, h)
            zero_onehot(BLOCKS - 1)
            scatter(BLOCKS - 1, 0)

            def gather_loop(ly):
                def gather(j):
                    g.indirect_dma_start(rows[j][:], None, support[ly.n],
                                         bass.IndirectOffsetOnAxis(ap=staged_index[:, j:j + 1], axis=0))\
                        .then_inc(ly.gathered[j], 16)
                for j in range(2):
                    pool.wait_ge(dense[ly.n].sup_stored[j], 16 * ((TILES - j + 1) // 2))
                for h in range(2):
                    pool.wait_ge(ly.index_staged, h + 1)
                    for j in range(h * H, h * H + H):
                        gather(j)
                with pool.Fori(1, PASSES) as it:
                    for h in range(2):
                        wait_alone(pool, ly.index_staged, it * 2 + (h + 1))
                        for j in range(h * H, h * H + H):
                            gather(j)

            gather_loop(layer[0])

            def zero_acc(t, j, n):
                wait_alone(pool, dense[1].x1_ready, t + 1)
                g.tensor_copy(tile_acc(t, P).rearrange("p (z w) -> p z w", z=KB), bcast(zeros[:, 0:P], 1, KB)).then_inc(acc_zeroed, 1)
            tiles_of(zero_acc)(pool)
            gather_loop(layer[1])

        @block.tensor
        def _(pe):
            mm = nc.tensor.matmul
            pe.wait_ge(constants, CONSTANTS)

            def count_block(b, bank_no, slot):
                pe.wait_ge(onehot_ready, b + 1)
                cols = bank[bank_no][:, bass.ds(slot * TW, TILES)]
                oh = onehot[:, bass.ds(b * OH, OH)].rearrange("p (k t) -> p k t", k=BC)
                for k in range(BC):
                    last = mm(cols, pick[:, P - 1 - k:2 * P - 1 - k], oh[:, k, :], start=(k == 0), stop=(k == BC - 1))
                last.then_inc(counted, 1)

            with pe.Fori(0, 10) as b:
                count_block(b, 0, b)
            with pe.Fori(10, BLOCKS) as b:
                count_block(b, 1, b - 10)

            pe.wait_ge(col_count_ready, 2)
            for b in range(BLOCKS):
                mm(bank[2][0:TILES, b:b + 1], col_count[:, b, 0:TILES], ones16[:], start=True, stop=True)\
                    .then_inc(tile_counts, 1)
            pe.wait_ge(unit_steps, 7)
            for b in range(BLOCKS):
                o = (b % 10) * TW
                mm(bank[3 + b // 10][:, o:o + TW], units_f[:, b:b + 1].to_broadcast([TILES, P]), tile_before[:],
                   start=True, stop=True).then_inc(starts_ready, 1)
            for b in range(BLOCKS):
                o = (b % 10) * TW
                at = bank[5 + b // 10][:, o:o + TW]
                mm(at, units_f[:, b:b + 1].to_broadcast([TILES, P]), tile_after_neg[:], start=True, stop=False)
                mm(at, units_before[:, b:b + 1].to_broadcast([TILES, P]), tile_same[:], start=False, stop=False)
                mm(at, chunks_f[:].to_broadcast([TILES, P]), tile_chunks[:], start=False, stop=True)\
                    .then_inc(starts_ready, 1)
            mm(bank[7][:, 0:TILES], chunks_f[:].to_broadcast([TILES, P]), tile_before[:, 1:TW],
               start=True, stop=True).then_inc(starts_ready, 1)

            pe.wait_ge(weights_loaded, 16 * (KB + 1))
            pe.wait_ge(col_count_ready, 2)
            for kb in range(KB):
                if kb >= 1:
                    pe.wait_ge(w0_copied, kb)
                for q in range(KB):
                    nc.tensor.transpose(bank[0][:, q * P:(q + 1) * P], wload[q][:, kb * P:(kb + 1) * P],
                                        ident[:]).then_inc(w0t_ready, 1)
            pe.wait_ge(w0_copied, KB)
            pe.wait_ge(starts_copied, 6)
            pe.wait_ge(dest_steps, 9)

            def dense_phase(d):
                def turn(t, n):
                    pe.wait_ge(d.hid_ready, t + 1)
                    if not isinstance(t, int) or t >= 2:
                        pe.wait_ge(d.hidt_ready, t - 1)
                    return n

                def turn_tile(t, j, n):
                    turn(t, n)
                    for q in range(KB):
                        last = nc.tensor.transpose(bank[j % 2][:, q * P:q * P + n], hid[j % 2][0:n, q * P:(q + 1) * P],
                                                   ident[0:n, 0:n])
                    last.then_inc(d.turned, 1)

                def product(t, j, n):
                    pe.wait_ge(d.hidt_ready, t + 1)
                    if not isinstance(t, int) or t >= 2:
                        pe.wait_ge(d.sup_ready, t - 1)
                    for q in range(KB):
                        last = mm(bank[2 + j % 2][0:n, :], hidt[j % 2][:, q * P:q * P + n], wt[d.n][:, q, :],
                                  start=(q == 0), stop=(q == KB - 1))
                    last.then_inc(d.product, 1)

                turn_tile(0, 0, P)

                def step(t, j):
                    turn_tile(t + 1, (j + 1) % 4, P)
                    product(t, j, P)
                for t in range(4):
                    step(t, t)
                with pe.Fori(1, TILES // 4 - 1) as it:
                    for j in range(4):
                        step(it * 4 + j, j)
                for t in range(TILES - 5, TILES - 2):
                    step(t, t % 4)
                turn_tile(TILES - 1, 0, LAST)
                product(TILES - 2, 3, P)
                product(TILES - 1, 0, LAST)

            dense_phase(dense[0])

            def ranks(b, h):
                for gr in range(GROUPS):
                    no = (GROUPS * h + gr) % 2
                    group = b * GROUPS + gr
                    if not isinstance(b, int) or group >= 2:
                        pe.wait_ge(ranked_done, group - 1)
                    else:
                        pe.wait_ge(dense[0].sup_ready, TILES)
                    at = bank[4 + no]
                    mm(at[0:EP, 0:GC * TILES], before[:], onehot[:, bass.ds(group * GC * TILES, GC * TILES)],
                       start=True, stop=False)
                    for i in range(GC):
                        k = gr * GC + i
                        last = mm(at[0:EP, i * TILES:(i + 1) * TILES], col_before[:, k:k + 1].to_broadcast([P, EP]),
                                  col_count[:, bass.ds(b, 1), 0:TILES].rearrange("p a t -> p (a t)"),
                                  start=False, stop=(i == GC - 1))
                    last.then_inc(rank_ready, 1)

            def permute(b, h):
                if not isinstance(b, int) or b >= 2:
                    pe.wait_ge(units_out, b * 2 - 2)
                for gr in range(GROUPS):
                    pe.wait_ge(perm_ready, b * GROUPS + (gr + 1))
                    for i in range(GC):
                        last = mm(bank[6 + h][:, 0:REC * C56], perm_row[(GROUPS * h + gr) % 2][:, i, :],
                                  perm_val[(GROUPS * h + gr) % 2][:, i, :, :].rearrange("p v c -> p (v c)"),
                                  start=(gr == 0 and i == 0), stop=(gr == GROUPS - 1 and i == GC - 1))
                    last.then_inc(permuted, 1)

            ranks(0, 0)
            ranks(1, 1)
            permute(0, 0)
            with pe.Fori(1, BLOCKS // 2) as it:
                ranks(it * 2, 0)
                permute(it * 2 - 1, 1)
                ranks(it * 2 + 1, 1)
                permute(it * 2, 0)
            ranks(BLOCKS - 1, 0)
            permute(BLOCKS - 2, 1)
            permute(BLOCKS - 1, 0)

            pe.wait_ge(rows_loaded, 16 * (TCHUNKS // P))
            for half in range(TCHUNKS // P // 4):
                for v in range(REC):
                    for i in range(4):
                        rec = chunk_rows[4 * half + i].rearrange("c (m v) -> c v m", v=REC)[:, v, :]
                        last = nc.tensor.transpose(bank[2 * half + v][:, i * P:(i + 1) * P], rec, ident[:])
                    last.then_inc(rows_turned, 1)

            def layer_loop(ly):
                def chunk(c, j, it):
                    pe.wait_ge(ly.sel_ready, c + 1)
                    pe.wait_ge(ly.gathered[j], it * 16 + 16)
                    if not isinstance(c, int) or c >= 4:
                        pe.wait_ge(ly.added, c - 3)
                    mm(bank[4 + j % 4][:], sel[:, j, :], rows[j][:], start=True, stop=True).then_inc(ly.summed, 1)
                for j in range(U):
                    chunk(j, j, 0)
                with pe.Fori(1, PASSES) as it:
                    for j in range(U):
                        chunk(it * U + j, j, it)

            layer_loop(layer[0])
            dense_phase(dense[1])
            layer_loop(layer[1])

        @block.vector
        def _(dve):
            v = nc.vector
            dve.wait_ge(edges_loaded, 48)
            v.tensor_scalar(edge_loc[:], edge_src[:], P - 1, None, ALU.bitwise_and).then_inc(prep, 1)
            dve.wait_ge(prep, 1)
            v.scalar_tensor_tensor(out=edge_dst[:], in0=edge_dst[:], scalar=7, in1=edge_loc[:],
                                   op0=ALU.logical_shift_left, op1=ALU.bitwise_or).then_inc(prep, 1)
            dve.wait_ge(prep, 2)
            v.tensor_scalar(edge_loc[:], edge_src[:], 7, None, ALU.logical_shift_right).then_inc(prep, 1)
            dve.wait_ge(prep, 3)
            v.tensor_copy(edge_tile, edge_loc[:]).then_inc(prep, 1)
            v.tensor_copy(edge_pack, edge_dst[:]).then_inc(prep, 1)
            dve.wait_ge(prep, 5)
            dve.wait_ge(constants, CONSTANTS)

            with dve.Fori(0, BLOCKS) as b:
                v.tensor_tensor(onehot[:, bass.ds(b * OH, OH)].rearrange("p (k t) -> p k t", k=BC),
                                bcast(edge_tile[:, bass.ds(b * BC, BC)], 2, TILES),
                                bcast(iota[0:EP, 0:TILES], 1, BC), ALU.is_equal).then_inc(onehot_ready, 1)

            dve.wait_ge(tile_counts, BLOCKS)
            steps = iter(range(1, 100))

            def counted_step(ins):
                n = next(steps)
                ins.then_inc(unit_steps, 1)
                dve.wait_ge(unit_steps, n)
            counted_step(v.tensor_scalar(units_i[:], bank[2][0:TILES, 0:BLOCKS], float(UNIT - 1), None, ALU.add))
            counted_step(v.tensor_scalar(units_i[:], units_i[:], 3, None, ALU.logical_shift_right))
            counted_step(v.tensor_copy(units_f[:], units_i[:]))
            counted_step(v.tensor_tensor_scan(units_to[:], units_f[:], zeros[0:TILES, 0:BLOCKS], 0.0,
                                              ALU.add, ALU.add))
            v.tensor_scalar(chunks_i[:], units_to[:, BLOCKS - 1:BLOCKS], float(CHUNK_UNITS - 1), None, ALU.add)\
                .then_inc(unit_steps, 1)
            next(steps)
            counted_step(v.tensor_tensor(units_before[:], units_to[:], units_f[:], ALU.subtract))
            v.tensor_scalar(chunks_i[:], chunks_i[:], 4, None, ALU.logical_shift_right).then_inc(prep, 1)
            dve.wait_ge(prep, 6)
            counted_step(v.tensor_copy(chunks_f[:], chunks_i[:]))

            dve.wait_ge(starts_copied, 6)

            def dest_step(n, ins):
                ins.then_inc(dest_steps, 1)
                dve.wait_ge(dest_steps, n)
            mask = unit_mask.rearrange("p (b u t) -> p b u t", b=BLOCKS, u=UCOLS)
            uid = bcast(unit_id[:], 1, BLOCKS)
            v.tensor_tensor(shift_step[:], unit_shift[:, :, 1:TW], unit_shift[:, :, 0:TILES], ALU.subtract)\
                .then_inc(dest_steps, 1)
            dest_step(2, v.tensor_tensor(mask, bcast(uid, 3, TILES), bcast(unit_start[:, :, 1:TW], 2, UCOLS),
                                         ALU.is_ge))
            dest_step(3, v.tensor_tensor(mask, mask, bcast(shift_step[:], 2, UCOLS), ALU.mult))
            dest_step(4, v.tensor_reduce(unit_dest[:], mask, AX.X, ALU.add))
            dest_step(5, v.tensor_tensor(unit_dest[:], unit_dest[:], uid, ALU.add))
            v.tensor_tensor(unit_dest_i[:].rearrange("p (b u) -> p b u", b=BLOCKS), unit_dest[:],
                            bcast(unit_shift[:, :, 0], 2, UCOLS), ALU.add).then_inc(dest_steps, 1)
            dest_step(7, v.tensor_tensor(chunk_mask[:], bcast(chunk_id[:], 2, TILES),
                                         bcast(chunk_start[:], 1, TCHUNKS // P), ALU.is_ge))
            dest_step(8, v.tensor_reduce(chunk_tile_f[:], chunk_mask[:, :, 0:TILES - 1], AX.X, ALU.add))
            dest_step(9, v.tensor_scalar(chunk_tile_i[:], chunk_tile_f[:], float(D), None, ALU.mult))

            def dense_phase(d):
                def norm(t, j, n, it):
                    dve.wait_ge(d.x_loaded[j], it * 16 + 16)
                    if d.n == 1:
                        v.tensor_tensor(xin[j][0:n, :], xin[j][0:n, :], tile_acc(t, n), ALU.add)\
                            .then_inc(d.x1_ready, 1)
                        dve.wait_ge(d.x1_ready, t + 1)
                    v.bn_stats(stats[0:n, j, :], xin[j][0:n, :]).then_inc(d.stats_done, 1)
                    wait_alone(dve, d.stats_done, t + 1)
                    v.bn_aggr(mv[0:n, j, :], stats[0:n, j, :]).then_inc(d.mv_ready, 1)
                    dve.wait_ge(d.std_ready, t + 1)
                    v.reciprocal(rstd[0:n, j, :], std[0:n, j, :]).then_inc(d.rstd_ready, 1)
                    dve.wait_ge(d.rstd_ready, t + 1)
                    v.tensor_scalar(nmr[0:n, j, :], mv[0:n, j, 0:1], rstd[0:n, j, :], -1.0, ALU.mult, ALU.mult)\
                        .then_inc(d.norm_ready, 1)

                def copy_turned(t, j, n):
                    dve.wait_ge(d.turned, t + 1)
                    if not isinstance(t, int) or t >= 2:
                        dve.wait_ge(d.product, t - 1)
                    v.tensor_copy(hidt[j % 2][:].rearrange("p (q m) -> p q m", q=KB)[:, :, 0:n],
                                  bank[j % 2][:].rearrange("p (q m) -> p q m", q=KB)[:, :, 0:n])\
                        .then_inc(d.hidt_ready, 1)

                def step(t, j, it):
                    norm(t + 1, (j + 1) % 4, P, it + (j + 1) // 4)
                    copy_turned(t, j, P)
                norm(0, 0, P, 0)
                for t in range(4):
                    step(t, t, 0)
                with dve.Fori(1, TILES // 4 - 1) as it:
                    for j in range(4):
                        step(it * 4 + j, j, it)
                for t in range(TILES - 5, TILES - 2):
                    step(t, t % 4, t // 4)
                norm(TILES - 1, 0, LAST, (TILES - 1) // 4)
                copy_turned(TILES - 2, 3, P)
                copy_turned(TILES - 1, 0, LAST)

            dense_phase(dense[0])

            def ranks(b, h):
                for gr in range(GROUPS):
                    no = (GROUPS * h + gr) % 2
                    group = b * GROUPS + gr
                    dve.wait_ge(rank_ready, group + 1)
                    v.tensor_tensor(ranked[no][:], bank[4 + no][0:EP, 0:GC * TILES].rearrange("p (k t) -> p k t", k=GC),
                                    onehot[:, bass.ds(group * GC * TILES, GC * TILES)]
                                    .rearrange("p (k t) -> p k t", k=GC), ALU.mult).then_inc(ranked_done, 1)
                    dve.wait_ge(ranked_done, group + 1)
                    v.tensor_reduce(place[:, gr * GC:(gr + 1) * GC], ranked[no][:], AX.X, ALU.add)\
                        .then_inc(placed, 1)
                dve.wait_ge(placed, b * GROUPS + GROUPS)
                v.tensor_copy(place_i[:], place[:]).then_inc(place_steps, 1)
                dve.wait_ge(place_steps, b * 5 + 1)
                v.tensor_scalar(prow_i[:], place_i[:], 3, P - 1, ALU.logical_shift_right, ALU.bitwise_and)\
                    .then_inc(place_steps, 1)
                v.tensor_scalar(pcol_i[:], place_i[:], 10, 3, ALU.logical_shift_right, ALU.logical_shift_left)\
                    .then_inc(place_steps, 1)
                dve.wait_ge(place_steps, b * 5 + 3)
                v.scalar_tensor_tensor(out=pcol_i[:], in0=place_i[:], scalar=UNIT - 1, in1=pcol_i[:],
                                       op0=ALU.bitwise_and, op1=ALU.bitwise_or).then_inc(place_steps, 1)
                v.tensor_copy(prow[h][:], prow_i[:]).then_inc(place_steps, 1)
                dve.wait_ge(place_steps, b * 5 + 5)
                v.tensor_copy(pcol[h][:], pcol_i[:]).then_inc(prep, 1)
                dve.wait_ge(prep, b + 7)

            def operands(b, h):
                for gr in range(GROUPS):
                    no = (GROUPS * h + gr) % 2
                    group = b * GROUPS + gr
                    c = bass.ds(group * GC, GC)
                    if not isinstance(b, int) or group >= 2:
                        dve.wait_ge(permuted, group - 1)
                    v.tensor_tensor(perm_col[no], bcast(iota[0:EP, 0:C56], 1, GC),
                                    bcast(pcol[h][:, gr * GC:(gr + 1) * GC], 2, C56), ALU.is_equal)\
                        .then_inc(perm_steps, 1)
                    v.tensor_tensor(perm_row[no], bcast(iota[0:EP, :], 1, GC),
                                    bcast(prow[h][:, gr * GC:(gr + 1) * GC], 2, P), ALU.is_equal)
                    dve.wait_ge(perm_steps, group + 1)
                    v.tensor_tensor(perm_val[no][:, :, 0, :], perm_col[no], bcast(edge_pack[:, c], 2, C56), ALU.mult)
                    v.tensor_tensor(perm_val[no][:, :, 1, :], perm_col[no], bcast(edge_w[:, c], 2, C56), ALU.mult)\
                        .then_inc(perm_ready, 1)

            ranks(0, 0)
            ranks(1, 1)
            operands(0, 0)
            with dve.Fori(1, BLOCKS // 2) as it:
                ranks(it * 2, 0)
                operands(it * 2 - 1, 1)
                ranks(it * 2 + 1, 1)
                operands(it * 2, 0)
            ranks(BLOCKS - 1, 0)
            operands(BLOCKS - 2, 1)
            operands(BLOCKS - 1, 0)

            for half in range(TCHUNKS // P // 4):
                s = slice(half * D, (half + 1) * D)
                dve.wait_ge(rows_turned, 2 * half + 1)
                v.tensor_copy(pack_i, bank[2 * half][:]).then_inc(table_steps, 1)
                dve.wait_ge(table_steps, 2 * half + 1)
                v.tensor_scalar(row_index[:, s], pack_i, 7, None, ALU.logical_shift_right).then_inc(table_ready, 1)
                v.tensor_scalar(loc_i, pack_i, P - 1, None, ALU.bitwise_and).then_inc(table_steps, 1)
                dve.wait_ge(table_steps, 2 * half + 2)
                v.tensor_copy(local_row[:, s], loc_i).then_inc(table_ready, 1)
            dve.wait_ge(table_ready, 6)
            dve.wait_ge(onehot_zeroed, BLOCKS + 1)
            dve.wait_ge(chunk_tile_in, 16)

            def layer_loop(ly):
                def select(c, j):
                    if not isinstance(c, int) or c >= U:
                        dve.wait_ge(ly.summed, c - (U - 1))
                    v.tensor_scalar(sel[:, j, :], iota[:], local_row[:, bass.ds(c, 1)], weight[:, bass.ds(c, 1)],
                                    ALU.is_equal, ALU.mult).then_inc(ly.sel_ready, 1)

                def add(c, j, where):
                    dve.wait_ge(ly.summed, c + 1)
                    if not isinstance(c, int) or c >= 1:
                        dve.wait_ge(ly.added, c)
                    at = acc[:, bass.ds(where, D)]
                    v.tensor_tensor(at, bank[4 + j % 4][:], at, ALU.add).then_inc(ly.added, 1)

                def tiles(it):
                    _, where = nc.values_load_multi_w_load_instructions(
                        chunk_tile[0:1, bass.ds(it * U, U)], engines=[DVE], min_val=0, max_val=(TILES - 1) * D,
                        skip_runtime_bounds_check_because="a count of at most TILES - 1 comparisons, times D")
                    return where

                def one(it):
                    where = tiles(it)
                    for j in range(U):
                        add(it * U + j, j, where[j])
                        select(it * U + (U + j), j)
                for j in range(U):
                    select(j, j)
                one(0)
                with dve.Fori(1, PASSES - 1) as it:
                    one(it)
                where = tiles(PASSES - 1)
                for j in range(U):
                    add((PASSES - 1) * U + j, j, where[j])

            layer_loop(layer[0])
            dve.wait_ge(layer[0].added, CHUNKS)
            dense_phase(dense[1])
            dve.wait_ge(acc_zeroed, TILES)
            layer_loop(layer[1])
            dve.wait_ge(layer[1].added, CHUNKS)

            def finish(t, j, n):
                if isinstance(t, int):
                    dve.wait_ge(fin_loaded[j], 16 * (t // 4) + 16)
                else:
                    dve.wait_ge(fin_loaded[j], (t - j) * 4 + 16)
                v.scalar_tensor_tensor(out=xin[j][0:n, :], in0=tile_acc(t, n), scalar=0.0, in1=xin[j][0:n, :],
                                       op0=ALU.max, op1=ALU.add).then_inc(fin_ready, 1)
            tiles_of(finish)(dve)

        @block.scalar
        def _(act):
            a = nc.scalar
            act.wait_ge(constants, CONSTANTS)
            act.wait_ge(counted, BLOCKS)
            for part, (lo, hi) in enumerate(((0, 10), (10, BLOCKS))):
                a.copy(col_count[:, lo:hi, 0:TILES],
                       bank[part][:, 0:(hi - lo) * TW].rearrange("p (b t) -> p b t", t=TW)[:, :, 0:TILES])\
                    .then_inc(col_count_ready, 1)
            act.wait_ge(starts_ready, 2 * BLOCKS + 1)
            act.wait_ge(tile_counts, BLOCKS)
            for part, (lo, hi) in enumerate(((0, 10), (10, BLOCKS))):
                w = (hi - lo) * TW
                a.copy(unit_start[:, lo:hi, :].rearrange("p b t -> p (b t)"), bank[3 + part][:, 0:w])\
                    .then_inc(starts_copied, 1)
                a.copy(col_count[64:65, lo:hi, :].rearrange("p b t -> p (b t)"), bank[3 + part][64:65, 0:w])\
                    .then_inc(col_count_ready, 1)
                a.copy(unit_shift[:, lo:hi, 0:TILES],
                       bank[5 + part][:, 0:w].rearrange("p (b t) -> p b t", t=TW)[:, :, 0:TILES])\
                    .then_inc(starts_copied, 1)
            a.copy(unit_shift[:, :, TILES], spill[:]).then_inc(starts_copied, 1)
            a.copy(chunk_start[:], bank[7][:, 0:TILES]).then_inc(starts_copied, 1)
            for kb in range(KB):
                act.wait_ge(w0t_ready, KB * (kb + 1))
                a.copy(wt[0][:, kb, :], bank[0][:]).then_inc(w0_copied, 1)

            def dense_phase(d):
                def norm(t, j, n):
                    act.wait_ge(d.mv_ready, t + 1)
                    a.activation(std[0:n, j, :], mv[0:n, j, 1:2], ACT.Sqrt, bias=eps[0:n, :]).then_inc(d.std_ready, 1)
                    act.wait_ge(d.norm_ready, t + 1)
                    if not isinstance(t, int) or t >= 2:
                        act.wait_ge(d.turned, t - 1)
                    a.activation(hid[j % 2][0:n, :], xin[j][0:n, :], ACT.Relu, bias=nmr[0:n, j, :],
                                 scale=rstd[0:n, j, :]).then_inc(d.hid_ready, 1)

                def store(t, j, n):
                    act.wait_ge(d.product, t + 1)
                    if not isinstance(t, int):
                        act.wait_ge(d.sup_stored[j % 2], (t - j % 2) * 8)
                    elif t >= 2:
                        act.wait_ge(d.sup_stored[j % 2], (t - t % 2) * 8)
                    a.copy(sup[j % 2][0:n, :], bank[2 + j % 2][0:n, :]).then_inc(d.sup_ready, 1)
                    act.wait_ge(d.sup_ready, t + 1)
                    act.dma_start(tile_rows(support[d.n], t, n), sup[j % 2][0:n, :])\
                        .then_inc(d.sup_stored[j % 2], 16)

                norm(0, 0, P)
                norm(1, 1, P)

                def step(t, j):
                    norm(t + 2, (j + 2) % 4, P)
                    store(t, j, P)
                for t in range(4):
                    step(t, t)
                with act.Fori(1, TILES // 4 - 1) as it:
                    for j in range(4):
                        step(it * 4 + j, j)
                for t in range(TILES - 5, TILES - 3):
                    step(t, t % 4)
                norm(TILES - 1, 0, LAST)
                for t in range(TILES - 3, TILES - 1):
                    store(t, t % 4, P)
                store(TILES - 1, 0, LAST)

            if True:
                act.wait_ge(w0t_ready, KB * KB)
                dense_phase(dense[0])

            act.wait_ge(dest_steps, 9)

            def units(b, h):
                act.wait_ge(permuted, b * GROUPS + GROUPS)
                if not isinstance(b, int):
                    act.wait_ge(scattered[h], (b - h) * (8 * UCOLS))
                elif b >= 2:
                    act.wait_ge(scattered[h], 16 * UCOLS * (b // 2))
                a.copy(unit_out[h][:], bank[6 + h][:, 0:REC * C56]
                       .rearrange("p (v c) -> p c v", v=REC)).then_inc(units_out, 1)
                a.copy(dest_now[h][:], unit_dest_i[:, bass.ds(b * UCOLS, UCOLS)]).then_inc(units_out, 1)
            units(0, 0)
            units(1, 1)
            with act.Fori(1, BLOCKS // 2) as it:
                for h in range(2):
                    units(it * 2 + h, h)
            units(BLOCKS - 1, 0)

            for half in range(TCHUNKS // P // 4):
                act.wait_ge(rows_turned, 2 * half + 2)
                a.copy(weight[:, half * D:(half + 1) * D], bank[2 * half + 1][:]).then_inc(table_ready, 1)
            act.wait_ge(table_ready, 6)

            def stage_indices(ly):
                for h in range(2):
                    a.copy(staged_index[:, h * H:(h + 1) * H], row_index[:, h * H:(h + 1) * H])\
                        .then_inc(ly.index_staged, 1)
                with act.Fori(1, PASSES) as it:
                    for h in range(2):
                        act.wait_ge(ly.summed, it * U + ((h + 1) * H - U))
                        a.copy(staged_index[:, h * H:(h + 1) * H], row_index[:, bass.ds(it * U + h * H, H)])\
                            .then_inc(ly.index_staged, 1)

            stage_indices(layer[0])
            dense_phase(dense[1])
            stage_indices(layer[1])

            def store_out(t, j, n):
                act.wait_ge(fin_ready, t + 1)
                act.dma_start(tile_rows(out, t, n), xin[j][0:n, :]).then_inc(fin_stored[j], 16)
            tiles_of(store_out)(act)
            for j in range(4):
                act.wait_ge(fin_stored[j], 16 * ((TILES - 1 - j) // 4 + 1))


def kernel(x, src, dst, edge_weight, L0_gnn_weight, L1_gnn_weight):
    import numpy as np
    import concourse.bacc as bacc
    from concourse.bass_utils import run_bass_kernel_spmd as run

    nc = bacc.Bacc("TRN2", target_bir_lowering=False, num_devices=1)
    arrays = {"x": x, "src": src, "dst": dst, "edge_weight": edge_weight, "w0": L0_gnn_weight, "w1": L1_gnn_weight}
    arrays = {f"in_{k}": np.ascontiguousarray(a) for k, a in arrays.items()}
    args = [nc.dram_tensor(k, a.shape, mybir.dt.from_np(a.dtype), kind="ExternalInput").ap()
            for k, a in arrays.items()]
    out = nc.dram_tensor("out_0", (NODES, D), F32, kind="ExternalOutput").ap()
    build_gnn(nc, *args, out)
    return run(nc, [arrays], core_ids=[0]).results[0]["out_0"]
```

```python
from contextlib import ExitStack

import concourse.bass as bass
from concourse import mybir
from concourse.alu_op_type import AluOpType as ALU

F32 = mybir.dt.float32
F16 = mybir.dt.float16
I32 = mybir.dt.int32
ACT = mybir.ActivationFunctionType
AX = mybir.AxisListType
DVE = mybir.EngineType.DVE

P = 128
NODES = 6250
D = 512
KB = D // P
EDGES = 106250
EPS = 1e-5

TILES = -(-NODES // P)
LAST = NODES - (TILES - 1) * P
EP = 125
EC = EDGES // EP
BC = 50
BLOCKS = EC // BC
GC = 10
GROUPS = BC // GC
BT = 3
SLOT_GROUP = (0, 2, 3)
UNIT_LOG = 2
UNIT = 1 << UNIT_LOG
REC = 2
UCOLS = -(-(-(-(EP * BC) // UNIT) + TILES) // P)
COLS = UCOLS * UNIT
BLOCK_UNITS = UCOLS * P
CHUNK_UNITS_LOG = 7 - UNIT_LOG
CHUNK_UNITS = 1 << CHUNK_UNITS_LOG
MAX_UNITS = (EDGES + (UNIT - 1) * BLOCKS * TILES) // UNIT
U = 12
H = 3
PARTS = U // H
CHUNKS = -(-((MAX_UNITS + TILES * (CHUNK_UNITS - 1)) // CHUNK_UNITS) // U) * U
PASSES = CHUNKS // U
SPAN = 18
USE_AT = 11
PART_AT = (2, 6, 9, 13)
TAIL_PART_AT = (2, 5, 8, 11)
BODY = 2 * SPAN
BODIES = CHUNKS // BODY - 1
SPREAD_CHUNKS = BODIES * BODY + U
TCHUNKS = -(-CHUNKS // P) * P
SPILL = CHUNKS * CHUNK_UNITS
OH = BC * TILES
ZW = OH // 2
ZR = 5
UROW = UNIT * REC
TABLE_ROWS = 3 * ZW * P // UROW
TW = TILES + 1
MASKS = 6
assert BT * (BLOCKS - 1) == TILES - 1 and EP * EC == EDGES and BLOCKS * BC == EC and GROUPS * GC == BC
assert BODY % U == 0 and SPAN == 6 * H and PARTS == 4 and 2 * BODIES + 1 == TILES and SPREAD_CHUNKS <= CHUNKS
assert OH % 2 == 0 and ZW % ZR == 0 and SPILL + BLOCKS * BLOCK_UNITS <= TABLE_ROWS
assert EP * BC + TILES * (UNIT - 1) <= BLOCK_UNITS * UNIT and TCHUNKS * CHUNK_UNITS <= TABLE_ROWS


def build_gnn(nc, x, src, dst, edge_weight, w0, w1, out):
    with ExitStack() as ctx:
        def sb(name, shape, dt):
            return ctx.enter_context(nc.sbuf_tensor(name, shape, dt))

        def bcast(ap, axis, n):
            shape = list(ap.shape)
            shape.insert(axis, n)
            return ap.unsqueeze(axis).to_broadcast(shape)

        def sem(name):
            return ctx.enter_context(nc.semaphore(name))

        table = nc.dram_tensor("sorted_units", [TABLE_ROWS, UROW], F32).ap()
        support = [nc.dram_tensor(f"support{n}", [NODES, D], F32).ap() for n in range(2)]
        x1_dram = nc.dram_tensor("x1", [NODES, D], F32).ap()
        col_count_dram = nc.dram_tensor("group_counts", [BLOCKS * GROUPS, GC * TILES], F16).ap()
        chunk_tile_dram = nc.dram_tensor("chunk_tile", [1, TCHUNKS], I32).ap()

        acc = sb("acc", [P, TILES * D], F32)
        onehot = acc[0:EP, 0:BLOCKS * OH // 2].bitcast(F16)
        row_ring = sb("row_ring", [P, U * D], F32)
        rows = [row_ring[:, j * D:(j + 1) * D] for j in range(U)]
        carved = [0]

        def carve(partitions, shape, dt):
            size = 1
            for n in shape:
                size *= n
            at, carved[0] = carved[0], carved[0] + size
            assert carved[0] <= U * D
            ap = row_ring[0:partitions, at:at + size]
            if dt != F32:
                ap = ap.bitcast(dt)
            if len(shape) == 2:
                ap = ap.rearrange("p (a b) -> p a b", a=shape[0])
            if len(shape) == 3:
                ap = ap.rearrange("p (a b c) -> p a b c", a=shape[0], b=shape[1])
            return ap

        work = sb("work", [P, 2 * GC * (P + COLS + REC * COLS)], F32)
        unit_mask = [work[:, u * BLOCKS * TILES:(u + 1) * BLOCKS * TILES].rearrange("p (b t) -> p b t", b=BLOCKS)
                     for u in range(MASKS)]
        group_count = work[0:BLOCKS * GROUPS, 0:GC * TILES // 2].bitcast(F16)
        start_term, after_term, before_term = [
            work[0:TILES, u * BLOCKS * TW:(u + 1) * BLOCKS * TW].rearrange("p (b t) -> p b t", b=BLOCKS)
            for u in range(3)]
        sel = work[:, 0:U * P].rearrange("p (j m) -> p j m", j=U)
        perm_row = [work[0:EP, h * GC * P:(h + 1) * GC * P].rearrange("p (k m) -> p k m", k=GC)
                    for h in range(2)]
        perm_col = [work[0:EP, 2 * GC * P + h * GC * COLS:2 * GC * P + (h + 1) * GC * COLS]
                    .rearrange("p (k m) -> p k m", k=GC) for h in range(2)]
        perm_val = [work[0:EP, 2 * GC * (P + COLS) + h * GC * REC * COLS:2 * GC * (P + COLS) + (h + 1) * GC * REC * COLS]
                    .rearrange("p (k v m) -> p k v m", k=GC, v=REC) for h in range(2)]
        row_index = sb("row_index", [P, TCHUNKS], I32)
        local_row = sb("local_row", [P, TCHUNKS], F32)
        weight = sb("weight", [P, TCHUNKS], F32)
        chunk_tile = sb("chunk_tile_sb", [1, TCHUNKS], I32)
        staged_index = sb("staged_index", [P, U], I32)
        wt = [sb(f"wt{n}", [P, KB, D], F32) for n in range(2)]
        xin = [sb(f"xin{j}", [P, D], F32) for j in range(4)]
        hid = [sb(f"hid{j}", [P, D], F32) for j in range(2)]
        hidt = [sb(f"hidt{j}", [P, D], F32) for j in range(2)]
        sup = [sb(f"sup{j}", [P, D], F32) for j in range(2)]
        stats = sb("stats", [P, 4, 6], F32)
        mv = sb("mv", [P, 4, 2], F32)
        std = sb("std", [P, 4, 1], F32)
        rstd = sb("rstd", [P, 4, 1], F32)
        nmr = sb("nmr", [P, 4, 1], F32)

        edge_src = carve(EP, [EC], I32)
        edge_dst = carve(EP, [EC], I32)
        edge_w = carve(EP, [EC], F32)
        edge_loc = carve(EP, [EC], I32)
        edge_tile = edge_loc.bitcast(F32)
        edge_pack = edge_src.bitcast(F32)
        place = sb("place", [EP, BC], F32)
        place_i = sb("place_i", [EP, BC], I32)
        prow_i = sb("prow_i", [EP, BC], I32)
        pcol_i = sb("pcol_i", [EP, BC], I32)
        prow = [sb(f"prow{h}", [EP, BC], F32) for h in range(2)]
        pcol = [sb(f"pcol{h}", [EP, BC], F32) for h in range(2)]
        ranked = [carve(EP, [GC, TILES], F32) for h in range(2)]
        col_count = sb("col_count", [P, BLOCKS, TW], F16)
        units_i = sb("units_i", [TILES, BLOCKS], I32)
        units_f = sb("units_f", [TILES, BLOCKS], F32)
        units_to = sb("units_to", [TILES, BLOCKS], F32)
        units_before = sb("units_before", [TILES, BLOCKS], F32)
        chunks_i = sb("chunks_i", [TILES, 1], I32)
        chunks_f = sb("chunks_f", [TILES, 1], F32)
        unit_start = weight[:, 0:BLOCKS * TW].rearrange("p (b t) -> p b t", b=BLOCKS)
        unit_shift = local_row[:, 0:BLOCKS * TW].rearrange("p (b t) -> p b t", b=BLOCKS)
        shift_step = carve(P, [BLOCKS, TILES], F32)
        unit_dest = sb("unit_dest", [P, BLOCKS, UCOLS], F32)
        unit_dest_i = sb("unit_dest_i", [P, BLOCKS * UCOLS], I32)
        chunk_mask = carve(P, [TCHUNKS // P, TILES], F32)
        chunk_start = sb("chunk_start", [P, TILES], F32)
        chunk_tile_f = sb("chunk_tile_f", [P, TCHUNKS // P], F32)
        chunk_tile_i = sb("chunk_tile_i", [P, TCHUNKS // P], I32)
        unit_out = [sb(f"unit_out{h}", [P, UCOLS * UNIT, REC], F32) for h in range(2)]
        dest_now = [sb(f"dest_now{h}", [P, UCOLS], I32) for h in range(2)]
        chunk_rows = [rows[g][:, 0:P * REC] for g in range(TCHUNKS // P)]
        pack_i = xin[0][:].bitcast(I32)
        loc_i = xin[1][:].bitcast(I32)
        wload = [[hid[0], hid[1], hidt[0], hidt[1]][q] for q in range(KB)]

        iota = sb("iota", [P, P], F32)
        unit_id = sb("unit_id", [P, UCOLS], F32)
        chunk_id = sb("chunk_id", [P, TCHUNKS // P], F32)
        spill = sb("spill", [P, BLOCKS], F32)
        before = sb("before", [EP, EP], F16)
        pick = sb("pick", [EP, 2 * P - 1], F16)
        col_before = sb("col_before", [P, BC], F16)
        ones16 = sb("ones16", [P, 1], F16)
        ones32 = sb("ones32", [TILES, 1], F32)
        tile_before = sb("tile_before", [TILES, TW], F32)
        tile_after_neg = sb("tile_after_neg", [TILES, TW], F32)
        tile_chunks = sb("tile_chunks", [TILES, TW], F32)
        tile_same = sb("tile_same", [TILES, TW], F32)
        ident = sb("ident", [P, P], F32)
        zeros = sb("zeros", [P, ZW // ZR], F32)
        zeros_wide = bcast(zeros[:], 1, ZR)
        eps = sb("eps", [P, 1], F32)
        chunk_limit = sb("chunk_limit", [1, TILES], F32)
        tile_late = sb("tile_late", [1, TILES], F32)
        late_f = sb("late_f", [1, 1], F32)
        late_i = sb("late_i", [1, 1], I32)

        bank = [ctx.enter_context(nc.psum_tensor(f"bank{i}", [P, D], F32)) for i in range(8)]

        block = ctx.enter_context(nc.Block())

        filled = sem("filled")
        constants = sem("constants")
        edges_loaded = sem("edges_loaded")
        weights_loaded = sem("weights_loaded")
        table_zeroed = sem("table_zeroed")
        prep = sem("prep")
        onehot_ready = sem("onehot_ready")
        counted = sem("counted")
        group_count_ready = sem("group_count_ready")
        col_count_out = sem("col_count_out")
        col_count_in = sem("col_count_in")
        col_start_ready = sem("col_start_ready")
        tile_counts = sem("tile_counts")
        unit_steps = sem("unit_steps")
        start_terms = sem("start_terms")
        starts_ready = sem("starts_ready")
        starts_copied = sem("starts_copied")
        dest_steps = sem("dest_steps")
        unit_masked = sem("unit_masked")
        unit_dest_done = sem("unit_dest_done")
        chunk_tile_out = sem("chunk_tile_out")
        chunk_tile_in = sem("chunk_tile_in")
        late_steps = sem("late_steps")
        w0t_ready = sem("w0t_ready")
        w0_copied = sem("w0_copied")
        rank_ready = sem("rank_ready")
        ranked_done = sem("ranked_done")
        placed = sem("placed")
        place_steps = sem("place_steps")
        perm_steps = sem("perm_steps")
        perm_ready = sem("perm_ready")
        permuted = sem("permuted")
        units_out = sem("units_out")
        scattered = [sem(f"scattered{h}") for h in range(2)]
        onehot_zeroed = sem("onehot_zeroed")
        rows_loaded = sem("rows_loaded")
        rows_turned = sem("rows_turned")
        table_steps = sem("table_steps")
        table_ready = sem("table_ready")

        class Dense:

            def __init__(self, n):
                self.n = n
                self.x_loaded = [sem(f"x_loaded{n}{j}") for j in range(4)]
                self.x1_ready = sem(f"x1_ready{n}")
                self.x1_stored = [sem(f"x1_stored{n}{j}") for j in range(4)]
                self.stats_done = sem(f"stats_done{n}")
                self.mv_ready = sem(f"mv_ready{n}")
                self.std_ready = sem(f"std_ready{n}")
                self.rstd_ready = sem(f"rstd_ready{n}")
                self.norm_ready = sem(f"norm_ready{n}")
                self.hid_ready = sem(f"hid_ready{n}")
                self.turned = sem(f"turned{n}")
                self.hidt_ready = sem(f"hidt_ready{n}")
                self.product = sem(f"product{n}")
                self.sup_ready = sem(f"sup_ready{n}")
                self.sup_stored = [sem(f"sup_stored{n}{j}") for j in range(2)]

        class Layer:

            def __init__(self, n):
                self.n = n
                self.index_staged = sem(f"index_staged{n}")
                self.gathered = [sem(f"gathered{n}_{j}") for j in range(U)]
                self.sel_ready = sem(f"sel_ready{n}")
                self.summed = sem(f"summed{n}")
                self.added = sem(f"added{n}")

        dense = [Dense(0), Dense(1)]
        layer = [Layer(0), Layer(1)]
        acc_zeroed = sem("acc_zeroed")
        fin_loaded = [sem(f"fin_loaded{j}") for j in range(4)]
        fin_ready = sem("fin_ready")
        fin_stored = [sem(f"fin_stored{j}") for j in range(4)]

        FILLS = 14
        CONSTANTS = 16

        def wait_alone(eng, signal, value):
            if isinstance(value, int):
                eng.wait_ge(signal, value)
            else:
                value = eng.to_reg(value)
                eng.wait_ge(filled, FILLS)
                eng.wait_ge(signal, value)

        def tiles_of(body):
            def run(eng):
                for t in range(4):
                    body(t, t, P)
                with eng.Fori(1, TILES // 4) as it:
                    for j in range(4):
                        body(it * 4 + j, j, P)
                body(TILES - 1, 0, LAST)
            return run

        def two_forms(eng, spread, general):
            eng.wait_ge(late_steps, 3)
            late = eng.value_load(late_i[0:1, 0:1], min_val=0, max_val=TILES)
            with eng.If(late < 1):
                spread()
            with eng.Else():
                general()

        def spans(eng, body):
            body(0)
            body(1)
            with eng.Fori(2, BODIES) as it:
                body(it)

        def rows_of(t):
            return LAST if isinstance(t, int) and t == TILES - 1 else P

        def tile_rows(dram, t, n):
            if isinstance(t, int):
                return dram[t * P:t * P + n, :]
            return dram[bass.ds(t * P, n), :]

        def tile_acc(t, n):
            if isinstance(t, int):
                return acc[0:n, t * D:(t + 1) * D]
            return acc[0:n, bass.ds(t * D, D)]

        @block.sync
        def _(sp):
            for buf, dram in ((edge_src, src), (edge_dst, dst), (edge_w, edge_weight)):
                sp.dma_start(buf[:], dram.rearrange("(p c) -> p c", p=EP)).then_inc(edges_loaded, 16)
            for q in range(KB):
                sp.dma_start(wload[q][:], w0[q * P:(q + 1) * P, :]).then_inc(weights_loaded, 16)
            sp.dma_start(wt[1][:], w1.rearrange("(q p) o -> p q o", p=P)).then_inc(weights_loaded, 16)
            sp.wait_ge(filled, FILLS)
            flat = table.rearrange("r c -> (r c)").rearrange("(q p w) -> q p w", q=3, p=P)
            for q in range(3):
                sp.dma_start(flat[q].rearrange("p (z w) -> p z w", z=ZR), zeros_wide).then_inc(table_zeroed, 16)

            def load_tiles(d, source, ring):
                def load(t, j, n):
                    if not isinstance(t, int) or t >= ring:
                        wait_alone(sp, d.hid_ready, t - (ring - 1))
                        if d.n == 1:
                            wait_alone(sp, d.x1_stored[j], (t - j) * 4)
                    sp.dma_start(xin[j][0:n, :], tile_rows(source, t, n)).then_inc(d.x_loaded[j], 16)
                return load

            def store_x1(t, j, n):
                d = dense[1]
                wait_alone(sp, d.x1_ready, t + 1)
                sp.dma_start(tile_rows(x1_dram, t, n), xin[j][0:n, :]).then_inc(d.x1_stored[j], 16)

            load = load_tiles(dense[0], x, BT)
            for t in range(BT):
                load(t, t, P)

            sp.wait_ge(group_count_ready, 1)
            sp.dma_start(col_count_dram, group_count).then_inc(col_count_out, 16)
            sp.wait_ge(col_count_out, 16)
            sp.wait_ge(filled, FILLS)
            sp.dma_start(col_count[0:BC, :, 0:TILES],
                         col_count_dram.rearrange("(b g) (c t) -> (g c) b t", g=GROUPS, t=TILES))\
                .then_inc(col_count_in, 16)

            sp.wait_ge(dest_steps, 6)
            sp.dma_start(chunk_tile_dram.rearrange("a (p j) -> (a p) j", p=P), chunk_tile_i[:])\
                .then_inc(chunk_tile_out, 16)
            sp.wait_ge(chunk_tile_out, 16)
            sp.dma_start(chunk_tile[:], chunk_tile_dram).then_inc(chunk_tile_in, 16)

            with sp.Fori(1, BLOCKS - 1) as b:
                for i in range(BT):
                    load(b * BT + i, i, P)
            load(TILES - 1, 0, LAST)

            sp.wait_ge(scattered[0], 16 * UCOLS * -(-BLOCKS // 2))
            sp.wait_ge(scattered[1], 16 * UCOLS * (BLOCKS // 2))
            by_chunk = table[0:TCHUNKS * CHUNK_UNITS, :].rearrange("(c u) r -> c (u r)", u=CHUNK_UNITS)
            for g in range(TCHUNKS // P):
                sp.dma_start(chunk_rows[g], by_chunk[g * P:(g + 1) * P, :]).then_inc(rows_loaded, 16)

            sp.wait_ge(table_ready, 6)

            def spread():
                d = dense[1]

                def tiles_in_turn(load, store):
                    load(0, 0, 0)
                    load(1, 1, 0)
                    with sp.Fori(0, BODIES - 1) as it:
                        for j in range(2):
                            store(it * 2 + j, j)
                            load(it * 2 + (j + 2), j, it + 1)
                    store(TILES - 3, 0)
                    load(TILES - 1, 0, BODIES)
                    store(TILES - 2, 1)
                    store(TILES - 1, 0)

                def load_x(t, j, uses):
                    if not isinstance(uses, int) or uses:
                        wait_alone(sp, d.hid_ready, t - 1)
                        wait_alone(sp, d.x1_stored[j], uses * 16)
                    sp.dma_start(xin[j][0:rows_of(t), :], tile_rows(x, t, rows_of(t))).then_inc(d.x_loaded[j], 16)

                def store_x1(t, j):
                    wait_alone(sp, d.x1_ready, t + 1)
                    sp.dma_start(tile_rows(x1_dram, t, rows_of(t)), xin[j][0:rows_of(t), :])\
                        .then_inc(d.x1_stored[j], 16)
                tiles_in_turn(load_x, store_x1)

                sp.wait_ge(d.hid_ready, TILES)
                for j in range(2):
                    sp.wait_ge(d.x1_stored[j], 16 * (BODIES + 1 - j))

                def load_x1(t, j, uses):
                    if not isinstance(uses, int) or uses:
                        wait_alone(sp, fin_stored[j], uses * 16)
                    sp.dma_start(xin[j][0:rows_of(t), :], tile_rows(x1_dram, t, rows_of(t)))\
                        .then_inc(fin_loaded[j], 16)

                def store_out(t, j):
                    wait_alone(sp, fin_ready, t + 1)
                    sp.dma_start(tile_rows(out, t, rows_of(t)), xin[j][0:rows_of(t), :]).then_inc(fin_stored[j], 16)
                tiles_in_turn(load_x1, store_out)
                for j in range(2):
                    sp.wait_ge(fin_stored[j], 16 * (BODIES + 1 - j))

            def general():
                load = load_tiles(dense[1], x, 4)

                def load_and_store(t, j, n):
                    load(t, j, n)
                    store_x1(t, j, n)
                load(0, 0, P)
                load(1, 1, P)

                def step(t, j):
                    load(t + 2, (j + 2) % 4, P)
                    store_x1(t, j, P)
                for t in range(4):
                    step(t, t)
                with sp.Fori(1, TILES // 4 - 1) as it:
                    for j in range(4):
                        step(it * 4 + j, j)
                for t in range(TILES - 5, TILES - 3):
                    step(t, t % 4)
                load(TILES - 1, 0, LAST)
                for t in range(TILES - 3, TILES - 1):
                    store_x1(t, t % 4, P)
                store_x1(TILES - 1, 0, LAST)

                sp.wait_ge(dense[1].hid_ready, TILES)
                for j in range(4):
                    sp.wait_ge(dense[1].x1_stored[j], 16 * ((TILES - 1 - j) // 4 + 1))

                def load_x1(t, j, n):
                    if not isinstance(t, int) or t >= 4:
                        wait_alone(sp, fin_stored[j], (t - j) * 4)
                    sp.dma_start(xin[j][0:n, :], tile_rows(x1_dram, t, n)).then_inc(fin_loaded[j], 16)
                tiles_of(load_x1)(sp)

            two_forms(sp, spread, general)

        @block.gpsimd
        def _(pool):
            g = nc.gpsimd
            for buf, value in ((before, 1.0), (pick, 0.0), (col_before, 1.0), (ones16, 1.0), (ones32, 1.0), (col_count, 0.0), (tile_before, 1.0),
                               (tile_after_neg, -1.0), (tile_chunks, float(CHUNK_UNITS)), (tile_same, 0.0),
                               (ident, 0.0), (zeros, 0.0), (eps, EPS)):
                g.memset(buf[:], value).then_inc(filled, 1)
            g.iota(unit_id[:], pattern=[[P, UCOLS]], base=0, channel_multiplier=1,
                   allow_small_or_imprecise_dtypes=True).then_inc(filled, 1)
            g.iota(iota[:], pattern=[[1, P]], base=0, channel_multiplier=0,
                   allow_small_or_imprecise_dtypes=True).then_inc(constants, 1)
            g.iota(chunk_id[:], pattern=[[1, TCHUNKS // P]], base=0, channel_multiplier=TCHUNKS // P,
                   allow_small_or_imprecise_dtypes=True).then_inc(constants, 1)
            g.iota(spill[:], pattern=[[BLOCK_UNITS, BLOCKS]], base=SPILL, channel_multiplier=0,
                   allow_small_or_imprecise_dtypes=True).then_inc(constants, 1)
            g.iota(chunk_limit[:], pattern=[[SPAN, TILES]], base=SPAN + USE_AT + 1, channel_multiplier=0,
                   allow_small_or_imprecise_dtypes=True).then_inc(constants, 1)
            pool.wait_ge(filled, FILLS)
            for buf in (before, tile_before, tile_after_neg, tile_chunks, col_before):
                g.affine_select(out=buf[:], in_=buf[:], compare_op=ALU.is_ge, fill=0.0, base=-1,
                                pattern=[[1, buf.shape[1]]], channel_multiplier=-1).then_inc(constants, 1)
            for buf in (tile_same, ident):
                g.affine_select(out=buf[:], in_=buf[:], compare_op=ALU.not_equal, fill=1.0, base=0,
                                pattern=[[1, buf.shape[1]]], channel_multiplier=-1).then_inc(constants, 1)
            g.affine_select(out=pick[:], in_=pick[:], compare_op=ALU.not_equal, fill=1.0, base=-(P - 1),
                            pattern=[[1, 2 * P - 1]], channel_multiplier=0).then_inc(constants, 1)
            pool.wait_ge(constants, 12)
            g.memset(col_before[64:65, :], float(UNIT)).then_inc(constants, 1)
            g.memset(chunk_limit[:, TILES - 1:TILES], float(SPREAD_CHUNKS)).then_inc(constants, 1)
            g.memset(tile_after_neg[:, TILES:TW], 0.0).then_inc(constants, 1)
            g.memset(tile_chunks[:, TILES:TW], 0.0).then_inc(constants, 1)
            pool.wait_ge(constants, CONSTANTS)

            def scatter(b, h):
                wait_alone(pool, units_out, b * 2 + 2)
                for u in range(UCOLS):
                    g.indirect_dma_start(
                        table, bass.IndirectOffsetOnAxis(ap=dest_now[h][:, u:u + 1], axis=0),
                        unit_out[h][:, u * UNIT:(u + 1) * UNIT, :].rearrange("p r v -> p (r v)"), None).then_inc(scattered[h], 16)

            def zero_onehot(b):
                wait_alone(pool, ranked_done, b * GROUPS + GROUPS)
                if isinstance(b, int):
                    g.tensor_copy(acc[:, b * ZW:(b + 1) * ZW].rearrange("p (z w) -> p z w", z=ZR), zeros_wide).then_inc(onehot_zeroed, 1)
                else:
                    g.tensor_copy(acc[:, bass.ds(b * ZW, ZW)].rearrange("p (z w) -> p z w", z=ZR), zeros_wide).then_inc(onehot_zeroed, 1)

            pool.wait_ge(table_zeroed, 48)
            g.memset(acc[:, BLOCKS * ZW:TILES * D], 0.0).then_inc(onehot_zeroed, 1)
            with pool.Fori(0, BLOCKS // 2) as it:
                for h in range(2):
                    zero_onehot(it * 2 + h)
                    scatter(it * 2 + h, h)
            zero_onehot(BLOCKS - 1)
            scatter(BLOCKS - 1, 0)

            def gather_loop(ly, passes):
                def gather(j):
                    g.indirect_dma_start(rows[j][:], None, support[ly.n],
                                         bass.IndirectOffsetOnAxis(ap=staged_index[:, j:j + 1], axis=0))\
                        .then_inc(ly.gathered[j], 16)
                for j in range(2):
                    pool.wait_ge(dense[ly.n].sup_stored[j], 16 * ((TILES - j + 1) // 2))
                for h in range(PARTS):
                    pool.wait_ge(ly.index_staged, h + 1)
                    for j in range(h * H, h * H + H):
                        gather(j)
                with pool.Fori(1, passes) as it:
                    for h in range(PARTS):
                        wait_alone(pool, ly.index_staged, it * PARTS + (h + 1))
                        for j in range(h * H, h * H + H):
                            gather(j)

            def zero_acc(t, j, n):
                wait_alone(pool, dense[1].x1_ready, t + 1)
                g.tensor_copy(tile_acc(t, P).rearrange("p (z w) -> p z w", z=KB), bcast(zeros[:, 0:P], 1, KB)).then_inc(acc_zeroed, 1)

            def spread():
                gather_loop(layer[0], SPREAD_CHUNKS // U)
                gather_loop(layer[1], SPREAD_CHUNKS // U)

            def general():
                gather_loop(layer[0], PASSES)
                tiles_of(zero_acc)(pool)
                gather_loop(layer[1], PASSES)

            two_forms(pool, spread, general)

        @block.tensor
        def _(pe):
            mm = nc.tensor.matmul
            pe.wait_ge(constants, CONSTANTS)

            def count_block(b, first=False, last=False):
                pe.wait_ge(onehot_ready, b + 1)
                for gr in range(GROUPS):
                    end = last and gr == GROUPS - 1
                    count = mm(bank[0][:, 0:GC * TILES], pick[:, bass.ds(P - 1 - gr - b * GROUPS, P)],
                               onehot[:, bass.ds(b * OH + gr * GC * TILES, GC * TILES)],
                               start=(first and gr == 0), stop=end)
                    if end:
                        count.then_inc(counted, 1)
            count_block(0, first=True)
            with pe.Fori(1, BLOCKS - 1) as b:
                count_block(b)
            count_block(BLOCKS - 1, last=True)

            pe.wait_ge(weights_loaded, 16 * (KB + 1))
            for kb in range(KB):
                if kb >= 1:
                    pe.wait_ge(w0_copied, kb)
                for q in range(KB):
                    nc.tensor.transpose(bank[1][:, q * P:(q + 1) * P], wload[q][:, kb * P:(kb + 1) * P],
                                        ident[:]).then_inc(w0t_ready, 1)

            pe.wait_ge(col_count_in, 16)
            for b in range(BLOCKS):
                mm(bank[2][0:TILES, b:b + 1], col_count[:, b, 0:TILES], ones16[:], start=True, stop=True)\
                    .then_inc(tile_counts, 1)
            halves = ((0, 10), (10, BLOCKS))
            ones = ones32[:].to_broadcast([TILES, P])
            pe.wait_ge(start_terms, 1)
            for part, (lo, hi) in enumerate(halves):
                mm(bank[3 + part][:, 0:(hi - lo) * TW], ones, start_term[:, lo:hi, :].rearrange("p b t -> p (b t)"),
                   start=True, stop=True).then_inc(starts_ready, 1)
            pe.wait_ge(start_terms, 3)
            for part, (lo, hi) in enumerate(halves):
                at = bank[5 + part][:, 0:(hi - lo) * TW]
                mm(at, ones, after_term[:, lo:hi, :].rearrange("p b t -> p (b t)"), start=True, stop=False)
                mm(at, ones, before_term[:, lo:hi, :].rearrange("p b t -> p (b t)"), start=False, stop=False)
                pe.wait_ge(unit_steps, 7)
                mm(at.rearrange("p (b t) -> p b t", t=TW), chunks_f[:].to_broadcast([TILES, P]),
                   bcast(tile_chunks[:], 1, hi - lo), start=False, stop=True).then_inc(starts_ready, 1)
            mm(bank[7][:, 0:TILES], chunks_f[:].to_broadcast([TILES, P]), tile_before[:, 1:TW],
               start=True, stop=True).then_inc(starts_ready, 1)
            pe.wait_ge(w0_copied, KB)
            pe.wait_ge(starts_copied, 6)
            pe.wait_ge(col_start_ready, 2)
            pe.wait_ge(dest_steps, 6)

            def turn_tile(d, t, j, n):
                pe.wait_ge(d.hid_ready, t + 1)
                if not isinstance(t, int) or t >= 2:
                    pe.wait_ge(d.hidt_ready, t - 1)
                for q in range(KB):
                    last = nc.tensor.transpose(bank[j % 2][:, q * P:q * P + n], hid[j % 2][0:n, q * P:(q + 1) * P],
                                               ident[0:n, 0:n])
                last.then_inc(d.turned, 1)

            def product_part(d, t, j, n, q):
                if q == 0:
                    pe.wait_ge(d.hidt_ready, t + 1)
                    if not isinstance(t, int) or t >= 2:
                        pe.wait_ge(d.sup_ready, t - 1)
                part = mm(bank[2 + j % 2][0:n, :], hidt[j % 2][:, q * P:q * P + n], wt[d.n][:, q, :],
                          start=(q == 0), stop=(q == KB - 1))
                if q == KB - 1:
                    part.then_inc(d.product, 1)

            def product(d, t, j, n):
                for q in range(KB):
                    product_part(d, t, j, n, q)

            def dense_phase(d):
                turn_tile(d, 0, 0, P)

                def step(t, j):
                    turn_tile(d, t + 1, (j + 1) % 4, P)
                    product(d, t, j, P)
                for t in range(4):
                    step(t, t)
                with pe.Fori(1, TILES // 4 - 1) as it:
                    for j in range(4):
                        step(it * 4 + j, j)
                for t in range(TILES - 5, TILES - 2):
                    step(t, t % 4)
                turn_tile(d, TILES - 1, 0, LAST)
                product(d, TILES - 2, 3, P)
                product(d, TILES - 1, 0, LAST)

            def rank(b, h, gr):
                no = (GROUPS * h + gr) % 2
                group = b * GROUPS + gr
                if not isinstance(b, int) or group >= 2:
                    pe.wait_ge(ranked_done, group - 1)
                at = bank[4 + no]
                mm(at[0:EP, 0:GC * TILES], before[:], onehot[:, bass.ds(group * GC * TILES, GC * TILES)],
                   start=True, stop=False)
                for i in range(GC):
                    k = gr * GC + i
                    last = mm(at[0:EP, i * TILES:(i + 1) * TILES], col_before[:, k:k + 1].to_broadcast([P, EP]),
                              col_count[:, bass.ds(b, 1), 0:TILES].rearrange("p a t -> p (a t)"),
                              start=False, stop=(i == GC - 1))
                last.then_inc(rank_ready, 1)

            def permute(b, h, gr):
                if gr == 0 and (not isinstance(b, int) or b >= 2):
                    pe.wait_ge(units_out, b * 2 - 2)
                no = (GROUPS * h + gr) % 2
                pe.wait_ge(perm_ready, b * GROUPS + (gr + 1))
                for i in range(GC):
                    last = mm(bank[6 + h][:, 0:REC * COLS], perm_row[no][:, i, :],
                              perm_val[no][:, i, :, :].rearrange("p v c -> p (v c)"),
                              start=(gr == 0 and i == 0), stop=(gr == GROUPS - 1 and i == GC - 1))
                last.then_inc(permuted, 1)

            def slot(t, j2):
                if not isinstance(t, int) or t < TILES:
                    turn_tile(dense[0], t, j2, P if not isinstance(t, int) or t < TILES - 1 else LAST)
                if not isinstance(t, int) or t >= 1:
                    product(dense[0], t - 1, 1 - j2, LAST if isinstance(t, int) and t == TILES else P)

            def sort_step(b, h, first=False, last=False):
                for gr in range(GROUPS):
                    if gr < GROUPS - 1 and not last:
                        rank(b, h, gr + 1)
                    if gr == GROUPS - 1 and not last and not (isinstance(b, int) and b == BLOCKS - 1):
                        rank(b + 1, 1 - h, 0)
                    for i in range(BT):
                        if SLOT_GROUP[i] == gr and not last and not (isinstance(b, int) and b * BT + i > TILES):
                            slot(b * BT + i, (h + i) % 2)
                    if not first:
                        permute(b - 1, 1 - h, gr)

            rank(0, 0, 0)
            sort_step(0, 0, first=True)
            sort_step(1, 1)
            with pe.Fori(1, BLOCKS // 2 - 1) as it:
                sort_step(it * 2, 0)
                sort_step(it * 2 + 1, 1)
            sort_step(BLOCKS - 3, 0)
            sort_step(BLOCKS - 2, 1)
            sort_step(BLOCKS - 1, 0)
            sort_step(BLOCKS, 1, last=True)

            pe.wait_ge(rows_loaded, 16 * (TCHUNKS // P))
            for half in range(TCHUNKS // P // 4):
                for v in range(REC):
                    for i in range(4):
                        rec = chunk_rows[4 * half + i].rearrange("c (m v) -> c v m", v=REC)[:, v, :]
                        last = nc.tensor.transpose(bank[2 * half + v][:, i * P:(i + 1) * P], rec, ident[:])
                    last.then_inc(rows_turned, 1)

            def chunk(ly, c, j, uses):
                pe.wait_ge(ly.sel_ready, c + 1)
                pe.wait_ge(ly.gathered[j], uses * 16 + 16)
                if not isinstance(c, int) or c >= 4:
                    pe.wait_ge(ly.added, c - 3)
                mm(bank[4 + j % 4][:], sel[:, j, :], rows[j][:], start=True, stop=True).then_inc(ly.summed, 1)

            def spread():
                def layer_spread(ly, d):
                    def body(it):
                        for k in range(2):
                            t = it * 2 + (k - 2)
                            dense_too = d is not None and (not isinstance(it, int) or t >= 0)
                            if dense_too:
                                turn_tile(d, t, k, P)
                            for i in range(SPAN):
                                at = k * SPAN + i
                                chunk(ly, it * BODY + at, at % U, it * (BODY // U) + at // U)
                                if dense_too and i in PART_AT:
                                    product_part(d, t, k, P, PART_AT.index(i))
                    spans(pe, body)
                    if d is not None:
                        turn_tile(d, TILES - 3, 0, P)
                    for j in range(U):
                        chunk(ly, BODIES * BODY + j, j, BODIES * (BODY // U))
                        if d is not None and j in TAIL_PART_AT:
                            product_part(d, TILES - 3, 0, P, TAIL_PART_AT.index(j))
                    if d is not None:
                        turn_tile(d, TILES - 2, 1, P)
                        turn_tile(d, TILES - 1, 0, LAST)
                        product(d, TILES - 2, 1, P)
                        product(d, TILES - 1, 0, LAST)
                layer_spread(layer[0], dense[1])
                layer_spread(layer[1], None)

            def general():
                def layer_loop(ly):
                    for j in range(U):
                        chunk(ly, j, j, 0)
                    with pe.Fori(1, PASSES) as it:
                        for j in range(U):
                            chunk(ly, it * U + j, j, it)
                layer_loop(layer[0])
                dense_phase(dense[1])
                layer_loop(layer[1])

            two_forms(pe, spread, general)

        @block.vector
        def _(dve):
            v = nc.vector
            dve.wait_ge(edges_loaded, 48)
            v.tensor_scalar(edge_loc[:], edge_src[:], P - 1, None, ALU.bitwise_and).then_inc(prep, 1)
            dve.wait_ge(prep, 1)
            v.scalar_tensor_tensor(out=edge_dst[:], in0=edge_dst[:], scalar=7, in1=edge_loc[:],
                                   op0=ALU.logical_shift_left, op1=ALU.bitwise_or).then_inc(prep, 1)
            dve.wait_ge(prep, 2)
            v.tensor_scalar(edge_loc[:], edge_src[:], 7, None, ALU.logical_shift_right).then_inc(prep, 1)
            dve.wait_ge(prep, 3)
            v.tensor_copy(edge_tile, edge_loc[:]).then_inc(prep, 1)
            v.tensor_copy(edge_pack, edge_dst[:]).then_inc(prep, 1)
            dve.wait_ge(prep, 5)
            dve.wait_ge(constants, CONSTANTS)

            with dve.Fori(0, BLOCKS) as b:
                v.tensor_tensor(onehot[:, bass.ds(b * OH, OH)].rearrange("p (k t) -> p k t", k=BC),
                                bcast(edge_tile[:, bass.ds(b * BC, BC)], 2, TILES),
                                bcast(iota[0:EP, 0:TILES], 1, BC), ALU.is_equal).then_inc(onehot_ready, 1)

            dve.wait_ge(tile_counts, BLOCKS)
            steps = iter(range(1, 100))

            def counted_step(ins):
                n = next(steps)
                ins.then_inc(unit_steps, 1)
                dve.wait_ge(unit_steps, n)
            counted_step(v.tensor_scalar(units_i[:], bank[2][0:TILES, 0:BLOCKS], float(UNIT - 1), None, ALU.add))
            counted_step(v.tensor_scalar(units_i[:], units_i[:], UNIT_LOG, None, ALU.logical_shift_right))
            counted_step(v.tensor_copy(units_f[:], units_i[:]))

            def term(out, per_block, per_tile):
                v.tensor_tensor(out, bcast(per_block[:], 2, TW), bcast(per_tile[:], 1, BLOCKS), ALU.mult)\
                    .then_inc(start_terms, 1)
            term(start_term, units_f, tile_before)
            counted_step(v.tensor_tensor_scan(units_to[:], units_f[:], zeros[0:TILES, 0:BLOCKS], 0.0,
                                              ALU.add, ALU.add))
            v.tensor_scalar(chunks_i[:], units_to[:, BLOCKS - 1:BLOCKS], float(CHUNK_UNITS - 1), None, ALU.add)\
                .then_inc(unit_steps, 1)
            next(steps)
            counted_step(v.tensor_tensor(units_before[:], units_to[:], units_f[:], ALU.subtract))
            term(before_term, units_before, tile_same)
            term(after_term, units_f, tile_after_neg)
            v.tensor_scalar(chunks_i[:], chunks_i[:], CHUNK_UNITS_LOG, None, ALU.logical_shift_right).then_inc(prep, 1)
            dve.wait_ge(prep, 6)
            counted_step(v.tensor_copy(chunks_f[:], chunks_i[:]))

            dve.wait_ge(starts_copied, 6)

            def dest_step(n, ins):
                ins.then_inc(dest_steps, 1)
                dve.wait_ge(dest_steps, n)
            uid = bcast(unit_id[:], 1, BLOCKS)
            dest_step(1, v.tensor_tensor(shift_step[:], unit_shift[:, :, 1:TW], unit_shift[:, :, 0:TILES],
                                         ALU.subtract))
            for first in range(0, UCOLS, MASKS):
                some = range(first, min(first + MASKS, UCOLS))
                if first:
                    dve.wait_ge(unit_dest_done, first)
                for u in some:
                    v.scalar_tensor_tensor(out=unit_mask[u - first], in0=unit_start[:, :, 1:TW],
                                           scalar=unit_id[:, u:u + 1], in1=shift_step[:],
                                           op0=ALU.is_le, op1=ALU.mult).then_inc(unit_masked, 1)
                for u in some:
                    dve.wait_ge(unit_masked, u + 1)
                    v.tensor_reduce(unit_dest[:, :, u], unit_mask[u - first], AX.X, ALU.add)\
                        .then_inc(unit_dest_done, 1)
            dve.wait_ge(unit_dest_done, UCOLS)
            dest_step(2, v.tensor_tensor(unit_dest[:], unit_dest[:], uid, ALU.add))
            v.tensor_tensor(unit_dest_i[:].rearrange("p (b u) -> p b u", b=BLOCKS), unit_dest[:],
                            bcast(unit_shift[:, :, 0], 2, UCOLS), ALU.add).then_inc(dest_steps, 1)
            dest_step(4, v.tensor_tensor(chunk_mask[:], bcast(chunk_id[:], 2, TILES),
                                         bcast(chunk_start[:], 1, TCHUNKS // P), ALU.is_ge))
            dest_step(5, v.tensor_reduce(chunk_tile_f[:], chunk_mask[:, :, 0:TILES - 1], AX.X, ALU.add))
            dest_step(6, v.tensor_scalar(chunk_tile_i[:], chunk_tile_f[:], float(D), None, ALU.mult))
            v.tensor_tensor(tile_late[:], chunk_start[0:1, :], chunk_limit[:], ALU.is_gt).then_inc(late_steps, 1)
            dve.wait_ge(late_steps, 1)
            v.tensor_reduce(late_f[:], tile_late[:], AX.X, ALU.add).then_inc(late_steps, 1)
            dve.wait_ge(late_steps, 2)
            v.tensor_copy(late_i[:], late_f[:]).then_inc(late_steps, 1)

            def statistics(d, t, j, n, use):
                dve.wait_ge(d.x_loaded[j], use * 16 + 16)
                if d.n == 1:
                    v.tensor_tensor(xin[j][0:n, :], xin[j][0:n, :], tile_acc(t, n), ALU.add)\
                        .then_inc(d.x1_ready, 1)
                    dve.wait_ge(d.x1_ready, t + 1)
                v.bn_stats(stats[0:n, j, :], xin[j][0:n, :]).then_inc(d.stats_done, 1)
                wait_alone(dve, d.stats_done, t + 1)
                v.bn_aggr(mv[0:n, j, :], stats[0:n, j, :]).then_inc(d.mv_ready, 1)

            def scales(d, t, j, n):
                dve.wait_ge(d.std_ready, t + 1)
                v.reciprocal(rstd[0:n, j, :], std[0:n, j, :]).then_inc(d.rstd_ready, 1)
                dve.wait_ge(d.rstd_ready, t + 1)
                v.tensor_scalar(nmr[0:n, j, :], mv[0:n, j, 0:1], rstd[0:n, j, :], -1.0, ALU.mult, ALU.mult)\
                    .then_inc(d.norm_ready, 1)

            def copy_turned(d, t, j, n):
                dve.wait_ge(d.turned, t + 1)
                if not isinstance(t, int) or t >= 2:
                    dve.wait_ge(d.product, t - 1)
                v.tensor_copy(hidt[j % 2][:].rearrange("p (q m) -> p q m", q=KB)[:, :, 0:n],
                              bank[j % 2][:].rearrange("p (q m) -> p q m", q=KB)[:, :, 0:n])\
                    .then_inc(d.hidt_ready, 1)

            def dense_phase(d):
                def norm(t, j, n, use):
                    statistics(d, t, j, n, use)
                    scales(d, t, j, n)

                def step(t, j, it):
                    norm(t + 1, (j + 1) % 4, P, it + (j + 1) // 4)
                    copy_turned(d, t, j, P)

                norm(0, 0, P, 0)
                for t in range(4):
                    step(t, t, 0)
                with dve.Fori(1, TILES // 4 - 1) as it:
                    for j in range(4):
                        step(it * 4 + j, j, it)
                for t in range(TILES - 5, TILES - 2):
                    step(t, t % 4, t // 4)
                norm(TILES - 1, 0, LAST, (TILES - 1) // 4)
                copy_turned(d, TILES - 2, 3, P)
                copy_turned(d, TILES - 1, 0, LAST)

            def rank(b, h, gr):
                no = (GROUPS * h + gr) % 2
                group = b * GROUPS + gr
                dve.wait_ge(rank_ready, group + 1)
                v.tensor_tensor(ranked[no][:], bank[4 + no][0:EP, 0:GC * TILES].rearrange("p (k t) -> p k t", k=GC),
                                onehot[:, bass.ds(group * GC * TILES, GC * TILES)]
                                .rearrange("p (k t) -> p k t", k=GC), ALU.mult).then_inc(ranked_done, 1)
                dve.wait_ge(ranked_done, group + 1)
                v.tensor_reduce(place[:, gr * GC:(gr + 1) * GC], ranked[no][:], AX.X, ALU.add).then_inc(placed, 1)

            def places(b, h):
                dve.wait_ge(placed, b * GROUPS + GROUPS)
                v.tensor_copy(place_i[:], place[:]).then_inc(place_steps, 1)
                dve.wait_ge(place_steps, b * 5 + 1)
                v.tensor_scalar(prow_i[:], place_i[:], UNIT_LOG, P - 1, ALU.logical_shift_right, ALU.bitwise_and)\
                    .then_inc(place_steps, 1)
                v.tensor_scalar(pcol_i[:], place_i[:], 7 + UNIT_LOG, UNIT_LOG, ALU.logical_shift_right,
                                ALU.logical_shift_left).then_inc(place_steps, 1)
                dve.wait_ge(place_steps, b * 5 + 3)
                v.scalar_tensor_tensor(out=pcol_i[:], in0=place_i[:], scalar=UNIT - 1, in1=pcol_i[:],
                                       op0=ALU.bitwise_and, op1=ALU.bitwise_or).then_inc(place_steps, 1)
                v.tensor_copy(prow[h][:], prow_i[:]).then_inc(place_steps, 1)
                dve.wait_ge(place_steps, b * 5 + 5)
                v.tensor_copy(pcol[h][:], pcol_i[:]).then_inc(prep, 1)
                dve.wait_ge(prep, b + 7)

            def operands(b, h, gr):
                no = (GROUPS * h + gr) % 2
                group = b * GROUPS + gr
                c = bass.ds(group * GC, GC)
                if not isinstance(b, int) or group >= 2:
                    dve.wait_ge(permuted, group - 1)
                v.tensor_tensor(perm_col[no], bcast(iota[0:EP, 0:COLS], 1, GC),
                                bcast(pcol[h][:, gr * GC:(gr + 1) * GC], 2, COLS), ALU.is_equal)\
                    .then_inc(perm_steps, 1)
                v.tensor_tensor(perm_row[no], bcast(iota[0:EP, :], 1, GC),
                                bcast(prow[h][:, gr * GC:(gr + 1) * GC], 2, P), ALU.is_equal)
                dve.wait_ge(perm_steps, group + 1)
                v.tensor_tensor(perm_val[no][:, :, 0, :], perm_col[no], bcast(edge_pack[:, c], 2, COLS), ALU.mult)
                v.tensor_tensor(perm_val[no][:, :, 1, :], perm_col[no], bcast(edge_w[:, c], 2, COLS), ALU.mult)\
                    .then_inc(perm_ready, 1)

            def slot(t, i):
                if not isinstance(t, int) or t + 1 < TILES:
                    scales(dense[0], t + 1, (i + 1) % BT, LAST if isinstance(t, int) and t + 1 == TILES - 1 else P)
                if isinstance(t, int) and t + 2 < TILES:
                    statistics(dense[0], t + 2, (i + 2) % BT, LAST if t + 2 == TILES - 1 else P, (t + 2) // BT)

            def sort_step(b, h, first=False, last=False):
                for gr in range(GROUPS):
                    for i in range(BT):
                        if SLOT_GROUP[i] == gr and not last:
                            slot(b * BT + i, i)
                            if not isinstance(b, int):
                                statistics(dense[0], b * BT + (i + 2), (i + 2) % BT, P, b + (i + 2) // BT)
                    if not last:
                        rank(b, h, gr)
                    if not first:
                        operands(b - 1, 1 - h, gr)
                if not last:
                    places(b, h)

            statistics(dense[0], 0, 0, P, 0)
            scales(dense[0], 0, 0, P)
            statistics(dense[0], 1, 1, P, 0)
            sort_step(0, 0, first=True)
            sort_step(1, 1)
            with dve.Fori(1, BLOCKS // 2 - 1) as it:
                sort_step(it * 2, 0)
                sort_step(it * 2 + 1, 1)
            sort_step(BLOCKS - 3, 0)
            sort_step(BLOCKS - 2, 1)
            sort_step(BLOCKS - 1, 0)
            sort_step(BLOCKS, 1, last=True)

            for half in range(TCHUNKS // P // 4):
                s = slice(half * D, (half + 1) * D)
                dve.wait_ge(rows_turned, 2 * half + 1)
                v.tensor_copy(pack_i, bank[2 * half][:]).then_inc(table_steps, 1)
                dve.wait_ge(table_steps, 2 * half + 1)
                v.tensor_scalar(row_index[:, s], pack_i, 7, None, ALU.logical_shift_right).then_inc(table_ready, 1)
                v.tensor_scalar(loc_i, pack_i, P - 1, None, ALU.bitwise_and).then_inc(table_steps, 1)
                dve.wait_ge(table_steps, 2 * half + 2)
                v.tensor_copy(local_row[:, s], loc_i).then_inc(table_ready, 1)
            dve.wait_ge(table_ready, 6)
            dve.wait_ge(onehot_zeroed, BLOCKS + 1)
            dve.wait_ge(chunk_tile_in, 16)

            def select(ly, c, j):
                if not isinstance(c, int) or c >= U:
                    dve.wait_ge(ly.summed, c - (U - 1))
                v.tensor_scalar(sel[:, j, :], iota[:], local_row[:, bass.ds(c, 1)], weight[:, bass.ds(c, 1)],
                                ALU.is_equal, ALU.mult).then_inc(ly.sel_ready, 1)

            def add(ly, c, j, where):
                dve.wait_ge(ly.summed, c + 1)
                if not isinstance(c, int) or c >= 1:
                    dve.wait_ge(ly.added, c)
                at = acc[:, bass.ds(where, D)]
                v.tensor_tensor(at, bank[4 + j % 4][:], at, ALU.add).then_inc(ly.added, 1)

            def places_of(first):
                _, where = nc.values_load_multi_w_load_instructions(
                    chunk_tile[0:1, bass.ds(first, U)], engines=[DVE], min_val=0, max_val=(TILES - 1) * D,
                    skip_runtime_bounds_check_because="a count of at most TILES - 1 comparisons, times D")
                return where

            def finish(t, j, n, uses):
                dve.wait_ge(fin_loaded[j], uses * 16 + 16)
                v.scalar_tensor_tensor(out=xin[j][0:n, :], in0=tile_acc(t, n), scalar=0.0, in1=xin[j][0:n, :],
                                       op0=ALU.max, op1=ALU.add).then_inc(fin_ready, 1)

            def spread():
                def layer_spread(ly, use, use_more):
                    def body(it):
                        for at in range(BODY):
                            k, i = at // SPAN, at % SPAN
                            if at % U == 0:
                                where = places_of(it * BODY + at)
                            add(ly, it * BODY + at, at % U, where[at % U])
                            select(ly, it * BODY + (at + U), at % U)
                            t = it * 2 + (k - 1)
                            if isinstance(it, int) and t < 0:
                                continue
                            if i == USE_AT:
                                dve.wait_ge(ly.added, it * BODY + (at + 1))
                                use(t, 1 - k, it + (k - 1))
                            if i == USE_AT + 2:
                                use_more(t, 1 - k)
                    for j in range(U):
                        select(ly, j, j)
                    spans(dve, body)
                    where = places_of(BODIES * BODY)
                    for j in range(U):
                        add(ly, BODIES * BODY + j, j, where[j])
                    dve.wait_ge(ly.added, SPREAD_CHUNKS)
                    use(TILES - 2, 1, BODIES - 1)
                    use(TILES - 1, 0, BODIES)
                    use_more(TILES - 2, 1)
                    use_more(TILES - 1, 0)

                d = dense[1]
                layer_spread(layer[0], lambda t, j, uses: statistics(d, t, j, rows_of(t), uses),
                             lambda t, j: scales(d, t, j, rows_of(t)))
                dve.wait_ge(acc_zeroed, TILES)
                layer_spread(layer[1], lambda t, j, uses: finish(t, j, rows_of(t), uses), lambda t, j: None)

            def general():
                def layer_loop(ly):
                    def one(it):
                        where = places_of(it * U)
                        for j in range(U):
                            add(ly, it * U + j, j, where[j])
                            select(ly, it * U + (U + j), j)
                    for j in range(U):
                        select(ly, j, j)
                    one(0)
                    with dve.Fori(1, PASSES - 1) as it:
                        one(it)
                    where = places_of((PASSES - 1) * U)
                    for j in range(U):
                        add(ly, (PASSES - 1) * U + j, j, where[j])
                    dve.wait_ge(ly.added, CHUNKS)

                layer_loop(layer[0])
                dense_phase(dense[1])
                dve.wait_ge(acc_zeroed, TILES)
                layer_loop(layer[1])
                for t in range(4):
                    finish(t, t, P, 0)
                with dve.Fori(1, TILES // 4) as it:
                    for j in range(4):
                        finish(it * 4 + j, j, P, it)
                finish(TILES - 1, 0, LAST, TILES // 4)

            two_forms(dve, spread, general)

        @block.scalar
        def _(act):
            a = nc.scalar
            act.wait_ge(constants, CONSTANTS)
            act.wait_ge(counted, 1)
            a.copy(group_count, bank[0][0:BLOCKS * GROUPS, 0:GC * TILES]).then_inc(group_count_ready, 1)
            for kb in range(KB):
                act.wait_ge(w0t_ready, KB * (kb + 1))
                a.copy(wt[0][:, kb, :], bank[1][:]).then_inc(w0_copied, 1)
            halves = ((0, 10), (10, BLOCKS))
            act.wait_ge(tile_counts, BLOCKS)
            act.wait_ge(starts_ready, 2)
            for part, (lo, hi) in enumerate(halves):
                w = (hi - lo) * TW
                a.copy(unit_start[:, lo:hi, :].rearrange("p b t -> p (b t)"), bank[3 + part][:, 0:w])\
                    .then_inc(starts_copied, 1)
                a.copy(col_count[64:65, lo:hi, :].rearrange("p b t -> p (b t)"), bank[3 + part][64:65, 0:w])\
                    .then_inc(col_start_ready, 1)
            act.wait_ge(starts_ready, 5)
            for part, (lo, hi) in enumerate(halves):
                w = (hi - lo) * TW
                a.copy(unit_shift[:, lo:hi, 0:TILES],
                       bank[5 + part][:, 0:w].rearrange("p (b t) -> p b t", t=TW)[:, :, 0:TILES])\
                    .then_inc(starts_copied, 1)
            a.copy(unit_shift[:, :, TILES], spill[:]).then_inc(starts_copied, 1)
            a.copy(chunk_start[:], bank[7][:, 0:TILES]).then_inc(starts_copied, 1)

            def root(d, t, j, n):
                act.wait_ge(d.mv_ready, t + 1)
                a.activation(std[0:n, j, :], mv[0:n, j, 1:2], ACT.Sqrt, bias=eps[0:n, :]).then_inc(d.std_ready, 1)

            def hidden(d, t, j, j2, n):
                act.wait_ge(d.norm_ready, t + 1)
                if not isinstance(t, int) or t >= 2:
                    act.wait_ge(d.turned, t - 1)
                a.activation(hid[j2][0:n, :], xin[j][0:n, :], ACT.Relu, bias=nmr[0:n, j, :],
                             scale=rstd[0:n, j, :]).then_inc(d.hid_ready, 1)

            def copy_turned(d, t, j2, n):
                act.wait_ge(d.turned, t + 1)
                if not isinstance(t, int) or t >= 2:
                    act.wait_ge(d.product, t - 1)
                a.copy(hidt[j2][:].rearrange("p (q m) -> p q m", q=KB)[:, :, 0:n],
                       bank[j2][:].rearrange("p (q m) -> p q m", q=KB)[:, :, 0:n]).then_inc(d.hidt_ready, 1)

            def store(d, t, j2, n):
                act.wait_ge(d.product, t + 1)
                if not isinstance(t, int):
                    act.wait_ge(d.sup_stored[j2], (t - j2) * 8)
                elif t >= 2:
                    act.wait_ge(d.sup_stored[j2], (t - j2) * 8)
                a.copy(sup[j2][0:n, :], bank[2 + j2][0:n, :]).then_inc(d.sup_ready, 1)
                act.wait_ge(d.sup_ready, t + 1)
                act.dma_start(tile_rows(support[d.n], t, n), sup[j2][0:n, :]).then_inc(d.sup_stored[j2], 16)

            def dense_phase(d):
                def norm(t, j, n):
                    root(d, t, j, n)
                    hidden(d, t, j, j % 2, n)

                norm(0, 0, P)
                norm(1, 1, P)

                def step(t, j):
                    norm(t + 2, (j + 2) % 4, P)
                    store(d, t, j % 2, P)
                for t in range(4):
                    step(t, t)
                with act.Fori(1, TILES // 4 - 1) as it:
                    for j in range(4):
                        step(it * 4 + j, j)
                for t in range(TILES - 5, TILES - 3):
                    step(t, t % 4)
                norm(TILES - 1, 0, LAST)
                for t in range(TILES - 3, TILES - 1):
                    store(d, t, t % 2, P)
                store(d, TILES - 1, 0, LAST)

            def units(b, h):
                act.wait_ge(permuted, b * GROUPS + GROUPS)
                if not isinstance(b, int):
                    act.wait_ge(scattered[h], (b - h) * (8 * UCOLS))
                elif b >= 2:
                    act.wait_ge(scattered[h], 16 * UCOLS * (b // 2))
                a.copy(unit_out[h][:], bank[6 + h][:, 0:REC * COLS]
                       .rearrange("p (v c) -> p c v", v=REC)).then_inc(units_out, 1)
                a.copy(dest_now[h][:], unit_dest_i[:, bass.ds(b * UCOLS, UCOLS)]).then_inc(units_out, 1)

            def slot(t, i, j2):
                d, some = dense[0], not isinstance(t, int)
                if some or t + 1 < TILES:
                    hidden(d, t + 1, (i + 1) % BT, 1 - j2, LAST if not some and t + 1 == TILES - 1 else P)
                if some or t < TILES:
                    copy_turned(d, t, j2, LAST if not some and t == TILES - 1 else P)
                if some or t + 2 < TILES:
                    root(d, t + 2, (i + 2) % BT, LAST if not some and t + 2 == TILES - 1 else P)
                if some or t >= 1:
                    store(d, t - 1, 1 - j2, LAST if not some and t == TILES else P)

            def sort_step(b, h, first=False, last=False):
                for i in range(BT):
                    if not last and not (isinstance(b, int) and b * BT + i > TILES):
                        slot(b * BT + i, i, (h + i) % 2)
                    if i == 0 and not (isinstance(b, int) and b < 2):
                        units(b - 2, h)
                if last:
                    units(BLOCKS - 1, 0)

            act.wait_ge(w0t_ready, KB * KB)
            act.wait_ge(dest_steps, 6)
            root(dense[0], 0, 0, P)
            hidden(dense[0], 0, 0, 0, P)
            root(dense[0], 1, 1, P)
            sort_step(0, 0, first=True)
            sort_step(1, 1)
            with act.Fori(1, BLOCKS // 2 - 1) as it:
                sort_step(it * 2, 0)
                sort_step(it * 2 + 1, 1)
            sort_step(BLOCKS - 3, 0)
            sort_step(BLOCKS - 2, 1)
            sort_step(BLOCKS - 1, 0)
            sort_step(BLOCKS, 1, last=True)

            for half in range(TCHUNKS // P // 4):
                act.wait_ge(rows_turned, 2 * half + 2)
                a.copy(weight[:, half * D:(half + 1) * D], bank[2 * half + 1][:]).then_inc(table_ready, 1)
            act.wait_ge(table_ready, 6)

            def stage(ly, first, h):
                if not isinstance(first, int) or first >= U:
                    act.wait_ge(ly.summed, first + (H - U))
                a.copy(staged_index[:, h * H:(h + 1) * H], row_index[:, bass.ds(first, H)]).then_inc(ly.index_staged, 1)

            def spread():
                d = dense[1]

                def zero_acc(t):
                    act.wait_ge(d.x1_ready, t + 1)
                    a.copy(tile_acc(t, P).rearrange("p (z w) -> p z w", z=KB), bcast(zeros[:, 0:P], 1, KB))\
                        .then_inc(acc_zeroed, 1)

                def layer_spread(ly, with_tiles):
                    def body(it):
                        for k in range(2):
                            t = it * 2 + (k - 1)
                            now = with_tiles and (not isinstance(it, int) or t >= 0)
                            before = with_tiles and (not isinstance(it, int) or t >= 1)
                            if before:
                                copy_turned(d, t - 1, k, P)
                            for m in range(6):
                                if m == 4 and now:
                                    root(d, t, 1 - k, P)
                                    zero_acc(t)
                                    hidden(d, t, 1 - k, 1 - k, P)
                                if m == 5 and before:
                                    store(d, t - 1, k, P)
                                stage(ly, it * BODY + (k * SPAN + U + m * H), (2 * k + m) % PARTS)
                    for h in range(PARTS):
                        stage(ly, h * H, h)
                    spans(act, body)
                    if with_tiles:
                        copy_turned(d, TILES - 3, 0, P)
                        store(d, TILES - 3, 0, P)
                        for t in range(TILES - 2, TILES):
                            root(d, t, t % 2, rows_of(t))
                        for t in range(TILES - 2, TILES):
                            hidden(d, t, t % 2, t % 2, rows_of(t))
                        for t in range(TILES - 2, TILES):
                            copy_turned(d, t, t % 2, rows_of(t))
                            zero_acc(t)
                        for t in range(TILES - 2, TILES):
                            store(d, t, t % 2, rows_of(t))
                layer_spread(layer[0], True)
                layer_spread(layer[1], False)

            def general():
                def stage_indices(ly):
                    for h in range(PARTS):
                        stage(ly, h * H, h)
                    with act.Fori(1, PASSES) as it:
                        for h in range(PARTS):
                            stage(ly, it * U + h * H, h)

                stage_indices(layer[0])
                dense_phase(dense[1])
                stage_indices(layer[1])

                def store_out(t, j, n):
                    act.wait_ge(fin_ready, t + 1)
                    act.dma_start(tile_rows(out, t, n), xin[j][0:n, :]).then_inc(fin_stored[j], 16)
                tiles_of(store_out)(act)
                for j in range(4):
                    act.wait_ge(fin_stored[j], 16 * ((TILES - 1 - j) // 4 + 1))

            two_forms(act, spread, general)


def kernel(x, src, dst, edge_weight, L0_gnn_weight, L1_gnn_weight):
    import numpy as np
    import concourse.bacc as bacc
    from concourse.bass_utils import run_bass_kernel_spmd as run

    nc = bacc.Bacc("TRN2", target_bir_lowering=False, num_devices=1)
    arrays = {"x": x, "src": src, "dst": dst, "edge_weight": edge_weight, "w0": L0_gnn_weight, "w1": L1_gnn_weight}
    arrays = {f"in_{k}": np.ascontiguousarray(a) for k, a in arrays.items()}
    args = [nc.dram_tensor(k, a.shape, mybir.dt.from_np(a.dtype), kind="ExternalInput").ap()
            for k, a in arrays.items()]
    out = nc.dram_tensor("out_0", (NODES, D), F32, kind="ExternalOutput").ap()
    build_gnn(nc, *args, out)
    return run(nc, [arrays], core_ids=[0]).results[0]["out_0"]
```

```python
from contextlib import ExitStack

import concourse.bass as bass
from concourse import mybir
from concourse.alu_op_type import AluOpType as ALU

F32 = mybir.dt.float32
F16 = mybir.dt.float16
I32 = mybir.dt.int32
ACT = mybir.ActivationFunctionType
AX = mybir.AxisListType
DVE = mybir.EngineType.DVE

P = 128
NODES = 6250
D = 512
KB = D // P
EDGES = 106250
EPS = 1e-5

TILES = -(-NODES // P)
LAST = NODES - (TILES - 1) * P
EP = 125
EC = EDGES // EP
BC = 50
BLOCKS = EC // BC
GC = 10
GROUPS = BC // GC
BT = 2
SLOT_GROUP = (0, 2)
EARLY = 16
COUNTING = 6
UNIT_LOG = 2
UNIT = 1 << UNIT_LOG
REC = 2
CHUNK_STARTS = 400
UCOLS = -(-(-(-(EP * BC) // UNIT) + TILES) // P)
COLS = UCOLS * UNIT
BLOCK_UNITS = UCOLS * P
CHUNK_UNITS_LOG = 7 - UNIT_LOG
CHUNK_UNITS = 1 << CHUNK_UNITS_LOG
MAX_UNITS = (EDGES + (UNIT - 1) * BLOCKS * TILES) // UNIT
U = 12
H = 3
PARTS = U // H
CHUNKS = -(-((MAX_UNITS + TILES * (CHUNK_UNITS - 1)) // CHUNK_UNITS) // U) * U
PASSES = CHUNKS // U
SPAN = 18
USE_AT = 11
PART_AT = (3, 7, 11, 15)
TAIL_PART_AT = (1, 2, 3, 4)
BODY = 2 * SPAN
BODIES = CHUNKS // BODY - 1
TAIL = 2 * H
SPREAD_CHUNKS = BODIES * BODY + TAIL
TCHUNKS = -(-CHUNKS // P) * P
SPILL = CHUNKS * CHUNK_UNITS
OH = BC * TILES
ZW = OH // 2
ZR = 5
UROW = UNIT * REC
TABLE_ROWS = 3 * ZW * P // UROW
TW = TILES + 1
MASKS = 6
assert EP * EC == EDGES and BLOCKS * BC == EC and GROUPS * GC == BC
assert EARLY + BT * BLOCKS == TILES + 1 and EARLY % 4 == 0 and 2 * COUNTING + 4 <= BLOCKS
assert COUNTING + 3 + (UCOLS + 1) // 2 == EARLY
assert EP * BC // UNIT + TILES <= 2048
assert BODY % U == 0 and SPAN == 6 * H and PARTS == 4 and 2 * BODIES + 1 == TILES and SPREAD_CHUNKS <= CHUNKS
assert OH % 2 == 0 and ZW % ZR == 0 and SPILL + BLOCKS * BLOCK_UNITS <= TABLE_ROWS
assert EP * BC + TILES * (UNIT - 1) <= BLOCK_UNITS * UNIT and TCHUNKS * CHUNK_UNITS <= TABLE_ROWS


def build_gnn(nc, x, src, dst, edge_weight, w0, w1, out):
    with ExitStack() as ctx:
        def sb(name, shape, dt):
            return ctx.enter_context(nc.sbuf_tensor(name, shape, dt))

        def bcast(ap, axis, n):
            shape = list(ap.shape)
            shape.insert(axis, n)
            return ap.unsqueeze(axis).to_broadcast(shape)

        def sem(name):
            return ctx.enter_context(nc.semaphore(name))

        table = nc.dram_tensor("sorted_units", [TABLE_ROWS, UROW], F32).ap()
        support = [nc.dram_tensor(f"support{n}", [NODES, D], F32).ap() for n in range(2)]
        x1_dram = nc.dram_tensor("x1", [NODES, D], F32).ap()
        col_count_dram = nc.dram_tensor("group_counts", [BLOCKS * GROUPS, GC * TILES], F16).ap()
        chunk_tile_dram = nc.dram_tensor("chunk_tile", [1, TCHUNKS], I32).ap()

        acc = sb("acc", [P, TILES * D], F32)
        onehot = acc[0:EP, 0:BLOCKS * OH // 2].bitcast(F16)
        row_ring = sb("row_ring", [P, U * D], F32)
        rows = [row_ring[:, j * D:(j + 1) * D] for j in range(U)]
        carved = [0]

        def carve(partitions, shape, dt):
            size = 1
            for n in shape:
                size *= n
            at, carved[0] = carved[0], carved[0] + size
            assert carved[0] <= U * D
            ap = row_ring[0:partitions, at:at + size]
            if dt != F32:
                ap = ap.bitcast(dt)
            if len(shape) == 2:
                ap = ap.rearrange("p (a b) -> p a b", a=shape[0])
            if len(shape) == 3:
                ap = ap.rearrange("p (a b c) -> p a b c", a=shape[0], b=shape[1])
            return ap

        work = sb("work", [P, 2 * GC * (P + COLS + REC * COLS)], F32)
        unit_mask = [work[:, u * BLOCKS * TILES:(u + 1) * BLOCKS * TILES].rearrange("p (b t) -> p b t", b=BLOCKS)
                     for u in range(MASKS)]
        group_count = work[0:BLOCKS * GROUPS, 0:GC * TILES // 2].bitcast(F16)
        start_term, after_term = [
            work[0:TILES, u * BLOCKS * TW // 2:(u + 1) * BLOCKS * TW // 2].bitcast(F16)
            .rearrange("p (b t) -> p b t", b=BLOCKS) for u in range(2)]
        before_term = work[0:TILES, BLOCKS * TW:2 * BLOCKS * TW].rearrange("p (b t) -> p b t", b=BLOCKS)
        sel = work[:, 0:U * P].rearrange("p (j m) -> p j m", j=U)
        perm_row = [work[0:EP, h * GC * P:(h + 1) * GC * P].rearrange("p (k m) -> p k m", k=GC)
                    for h in range(2)]
        perm_col = [work[0:EP, 2 * GC * P + h * GC * COLS:2 * GC * P + (h + 1) * GC * COLS]
                    .rearrange("p (k m) -> p k m", k=GC) for h in range(2)]
        perm_val = [work[0:EP, 2 * GC * (P + COLS) + h * GC * REC * COLS:2 * GC * (P + COLS) + (h + 1) * GC * REC * COLS]
                    .rearrange("p (k v m) -> p k v m", k=GC, v=REC) for h in range(2)]
        row_index = sb("row_index", [P, TCHUNKS], I32)
        local_row = sb("local_row", [P, TCHUNKS], F32)
        weight = sb("weight", [P, TCHUNKS], F32)
        chunk_tile = sb("chunk_tile_sb", [1, TCHUNKS], I32)
        staged_index = sb("staged_index", [P, U], I32)
        wt = [sb(f"wt{n}", [P, KB, D], F32) for n in range(2)]
        xin = [sb(f"xin{j}", [P, D], F32) for j in range(4)]
        hid = [sb(f"hid{j}", [P, D], F32) for j in range(2)]
        hidt = [sb(f"hidt{j}", [P, D], F32) for j in range(2)]
        sup = [sb(f"sup{j}", [P, D], F32) for j in range(2)]
        stats = sb("stats", [P, 4, 6], F32)
        mv = sb("mv", [P, 4, 2], F32)
        std = sb("std", [P, 4, 1], F32)
        rstd = sb("rstd", [P, 4, 1], F32)
        nmr = sb("nmr", [P, 4, 1], F32)

        edge_src = carve(EP, [EC], I32)
        edge_dst = carve(EP, [EC], I32)
        edge_w = carve(EP, [EC], F32)
        edge_loc = carve(EP, [EC], I32)
        edge_tile = edge_loc.bitcast(F32)
        edge_pack = edge_src.bitcast(F32)
        place = sb("place", [EP, BC], F32)
        place_i = sb("place_i", [EP, BC], I32)
        prow_i = sb("prow_i", [EP, BC], I32)
        pcol_i = sb("pcol_i", [EP, BC], I32)
        prow = [sb(f"prow{h}", [EP, BC], F32) for h in range(2)]
        pcol = [sb(f"pcol{h}", [EP, BC], F32) for h in range(2)]
        ranked = [carve(EP, [GC, TILES], F32) for h in range(2)]
        col_count = sb("col_count", [P, BLOCKS, TW], F16)
        units_i = sb("units_i", [TILES, BLOCKS], I32)
        units_f = sb("units_f", [TILES, BLOCKS], F32)
        units_to = sb("units_to", [TILES, BLOCKS], F32)
        units_before = sb("units_before", [TILES, BLOCKS], F32)
        chunks_i = sb("chunks_i", [TILES, 1], I32)
        chunks_f = sb("chunks_f", [TILES, 1], F32)
        unit_start = weight[:, 0:BLOCKS * TW].rearrange("p (b t) -> p b t", b=BLOCKS)
        unit_shift = local_row[:, 0:BLOCKS * TW].rearrange("p (b t) -> p b t", b=BLOCKS)
        shift_step = carve(P, [BLOCKS, TILES], F32)
        unit_dest = sb("unit_dest", [P, BLOCKS, UCOLS], F32)
        unit_dest_i = sb("unit_dest_i", [P, BLOCKS * UCOLS], I32)
        chunk_mask = carve(P, [TCHUNKS // P, TILES], F32)
        chunk_start = sb("chunk_start", [P, TILES], F32)
        chunk_tile_f = sb("chunk_tile_f", [P, TCHUNKS // P], F32)
        chunk_tile_i = sb("chunk_tile_i", [P, TCHUNKS // P], I32)
        unit_out = [sb(f"unit_out{h}", [P, UCOLS * UNIT, REC], F32) for h in range(2)]
        dest_now = [sb(f"dest_now{h}", [P, UCOLS], I32) for h in range(2)]
        chunk_rows = [rows[g if g < 4 else g + U - 8][:, 0:P * REC] for g in range(TCHUNKS // P)]
        pack_i = xin[0][:].bitcast(I32)
        loc_i = xin[1][:].bitcast(I32)
        wload = [[hid[0], hid[1], hidt[0], hidt[1]][q] for q in range(KB)]

        iota = sb("iota", [P, P], F32)
        unit_id = sb("unit_id", [P, UCOLS], F32)
        chunk_id = sb("chunk_id", [P, TCHUNKS // P], F32)
        spill = sb("spill", [P, BLOCKS], F32)
        before = sb("before", [EP, EP], F16)
        pick = sb("pick", [EP, 2 * P - 1], F16)
        col_before = sb("col_before", [P, BC], F16)
        ones16 = sb("ones16", [P, 1], F16)
        ones32 = sb("ones32", [TILES, 1], F32)
        tile_before = sb("tile_before", [TILES, TW], F32)
        tile_after_neg = sb("tile_after_neg", [TILES, TW], F32)
        tile_chunks = sb("tile_chunks", [TILES, TW], F32)
        tile_same = sb("tile_same", [TILES, TW], F32)
        ident = sb("ident", [P, P], F32)
        zeros = sb("zeros", [P, ZW // ZR], F32)
        zeros_wide = bcast(zeros[:], 1, ZR)
        eps = sb("eps", [P, 1], F32)
        chunk_limit = sb("chunk_limit", [1, TILES], F32)
        tile_late = sb("tile_late", [1, TILES], F32)
        late_f = sb("late_f", [1, 1], F32)
        late_i = sb("late_i", [1, 1], I32)

        bank = [ctx.enter_context(nc.psum_tensor(f"bank{i}", [P, D], F32)) for i in range(8)]

        block = ctx.enter_context(nc.Block())

        filled = sem("filled")
        constants = sem("constants")
        edges_loaded = sem("edges_loaded")
        weights_loaded = sem("weights_loaded")
        table_zeroed = sem("table_zeroed")
        prep = sem("prep")
        onehot_ready = sem("onehot_ready")
        counted = sem("counted")
        group_count_ready = sem("group_count_ready")
        col_count_out = sem("col_count_out")
        col_count_in = sem("col_count_in")
        col_start_ready = sem("col_start_ready")
        tile_counts = sem("tile_counts")
        unit_steps = sem("unit_steps")
        start_terms = sem("start_terms")
        starts_ready = sem("starts_ready")
        starts_copied = sem("starts_copied")
        dest_steps = sem("dest_steps")
        unit_masked = sem("unit_masked")
        unit_dest_done = sem("unit_dest_done")
        chunk_tile_out = sem("chunk_tile_out")
        chunk_tile_in = sem("chunk_tile_in")
        late_steps = sem("late_steps")
        w0t_ready = sem("w0t_ready")
        w0_copied = sem("w0_copied")
        rank_ready = sem("rank_ready")
        ranked_done = sem("ranked_done")
        placed = sem("placed")
        place_steps = sem("place_steps")
        perm_steps = sem("perm_steps")
        perm_ready = sem("perm_ready")
        perm_weighted = sem("perm_weighted")
        permuted = sem("permuted")
        units_out = sem("units_out")
        scattered = [sem(f"scattered{h}") for h in range(2)]
        onehot_zeroed = sem("onehot_zeroed")
        rows_loaded = [sem(f"rows_loaded{half}") for half in range(2)]
        rows_turned = sem("rows_turned")
        table_steps = sem("table_steps")
        table_ready = [sem(f"table_ready{half}") for half in range(2)]

        class Dense:

            def __init__(self, n):
                self.n = n
                self.x_loaded = [sem(f"x_loaded{n}{j}") for j in range(4)]
                self.x1_ready = sem(f"x1_ready{n}")
                self.x1_stored = [sem(f"x1_stored{n}{j}") for j in range(4)]
                self.stats_done = sem(f"stats_done{n}")
                self.mv_ready = sem(f"mv_ready{n}")
                self.std_ready = sem(f"std_ready{n}")
                self.rstd_ready = sem(f"rstd_ready{n}")
                self.norm_ready = sem(f"norm_ready{n}")
                self.hid_ready = sem(f"hid_ready{n}")
                self.turned = sem(f"turned{n}")
                self.hidt_ready = sem(f"hidt_ready{n}")
                self.product = sem(f"product{n}")
                self.sup_ready = sem(f"sup_ready{n}")
                self.sup_stored = [sem(f"sup_stored{n}{j}") for j in range(2)]

        class Layer:

            def __init__(self, n):
                self.n = n
                self.index_staged = sem(f"index_staged{n}")
                self.gathered = [sem(f"gathered{n}_{j}") for j in range(U)]
                self.sel_ready = sem(f"sel_ready{n}")
                self.summed = sem(f"summed{n}")
                self.added = sem(f"added{n}")

        dense = [Dense(0), Dense(1)]
        layer = [Layer(0), Layer(1)]
        acc_zeroed = sem("acc_zeroed")
        fin_loaded = [sem(f"fin_loaded{j}") for j in range(4)]
        fin_ready = sem("fin_ready")
        fin_stored = [sem(f"fin_stored{j}") for j in range(4)]

        FILLS = 14
        CONSTANTS = 17

        def wait_alone(eng, signal, value):
            if isinstance(value, int):
                eng.wait_ge(signal, value)
            else:
                value = eng.to_reg(value)
                eng.wait_ge(filled, FILLS)
                eng.wait_ge(signal, value)

        def tiles_of(body):
            def run(eng):
                for t in range(4):
                    body(t, t, P)
                with eng.Fori(1, TILES // 4) as it:
                    for j in range(4):
                        body(it * 4 + j, j, P)
                body(TILES - 1, 0, LAST)
            return run

        def two_forms(eng, spread, general):
            eng.wait_ge(late_steps, 3)
            late = eng.value_load(late_i[0:1, 0:1], min_val=0, max_val=TILES)
            with eng.If(late < 1):
                spread()
            with eng.Else():
                general()

        def spans(eng, body):
            body(0)
            body(1)
            with eng.Fori(2, BODIES) as it:
                body(it)

        def rows_of(t):
            return LAST if isinstance(t, int) and t == TILES - 1 else P

        def tile_rows(dram, t, n):
            if isinstance(t, int):
                return dram[t * P:t * P + n, :]
            return dram[bass.ds(t * P, n), :]

        def tile_acc(t, n):
            if isinstance(t, int):
                return acc[0:n, t * D:(t + 1) * D]
            return acc[0:n, bass.ds(t * D, D)]

        @block.sync
        def _(sp):
            for buf, dram in ((edge_src, src), (edge_dst, dst), (edge_w, edge_weight)):
                sp.dma_start(buf[:], dram.rearrange("(p c) -> p c", p=EP)).then_inc(edges_loaded, 16)
            for q in range(KB):
                sp.dma_start(wload[q][:], w0[q * P:(q + 1) * P, :]).then_inc(weights_loaded, 16)
            sp.dma_start(wt[1][:], w1.rearrange("(q p) o -> p q o", p=P)).then_inc(weights_loaded, 16)
            def load_tiles(d, source):
                def load(t, j, n):
                    if not isinstance(t, int) or t >= 4:
                        wait_alone(sp, d.hid_ready, t - 3)
                        if d.n == 1:
                            wait_alone(sp, d.x1_stored[j], (t - j) * 4)
                    sp.dma_start(xin[j][0:n, :], tile_rows(source, t, n)).then_inc(d.x_loaded[j], 16)
                return load

            def store_x1(t, j, n):
                d = dense[1]
                wait_alone(sp, d.x1_ready, t + 1)
                sp.dma_start(tile_rows(x1_dram, t, n), xin[j][0:n, :]).then_inc(d.x1_stored[j], 16)

            load = load_tiles(dense[0], x)
            for t in range(4):
                load(t, t, P)
            sp.wait_ge(filled, FILLS)
            flat = table.rearrange("r c -> (r c)").rearrange("(q p w) -> q p w", q=3, p=P)
            for q in range(3):
                sp.dma_start(flat[q].rearrange("p (z w) -> p z w", z=ZR), zeros_wide).then_inc(table_zeroed, 16)

            for t in range(4, COUNTING + 5):
                load(t, t % 4, P)

            sp.wait_ge(group_count_ready, 1)
            sp.dma_start(col_count_dram, group_count).then_inc(col_count_out, 16)
            sp.wait_ge(col_count_out, 16)
            sp.wait_ge(filled, FILLS)
            sp.dma_start(col_count[0:BC, :, 0:TILES],
                         col_count_dram.rearrange("(b g) (c t) -> (g c) b t", g=GROUPS, t=TILES))\
                .then_inc(col_count_in, 16)

            for t in range(COUNTING + 5, EARLY + 2):
                load(t, t % 4, P)
            sp.wait_ge(dest_steps, 6)
            sp.dma_start(chunk_tile_dram.rearrange("a (p j) -> (a p) j", p=P), chunk_tile_i[:])\
                .then_inc(chunk_tile_out, 16)
            sp.wait_ge(chunk_tile_out, 16)
            sp.dma_start(chunk_tile[:], chunk_tile_dram).then_inc(chunk_tile_in, 16)

            with sp.Fori(EARLY // 4, TILES // 4 - 1) as it:
                for j in range(4):
                    load(it * 4 + (j + 2), (j + 2) % 4, P)
            load(TILES - 3, 2, P)
            load(TILES - 2, 3, P)
            load(TILES - 1, 0, LAST)

            sp.wait_ge(scattered[0], 16 * UCOLS * -(-BLOCKS // 2))
            sp.wait_ge(scattered[1], 16 * UCOLS * (BLOCKS // 2))
            by_chunk = table[0:TCHUNKS * CHUNK_UNITS, :].rearrange("(c u) r -> c (u r)", u=CHUNK_UNITS)
            for g in range(TCHUNKS // P):
                sp.dma_start(chunk_rows[g], by_chunk[g * P:(g + 1) * P, :]).then_inc(rows_loaded[g // 4], 16)

            for half in range(2):
                sp.wait_ge(table_ready[half], 3)

            def spread():
                d = dense[1]

                def tiles_in_turn(load, store):
                    load(0, 0, 0)
                    load(1, 1, 0)
                    with sp.Fori(0, BODIES - 1) as it:
                        for j in range(2):
                            store(it * 2 + j, j)
                            load(it * 2 + (j + 2), j, it + 1)
                    store(TILES - 3, 0)
                    load(TILES - 1, 0, BODIES)
                    store(TILES - 2, 1)
                    store(TILES - 1, 0)

                def load_x(t, j, uses):
                    if not isinstance(uses, int) or uses:
                        wait_alone(sp, d.hid_ready, t - 1)
                        wait_alone(sp, d.x1_stored[j], uses * 16)
                    sp.dma_start(xin[j][0:rows_of(t), :], tile_rows(x, t, rows_of(t))).then_inc(d.x_loaded[j], 16)

                def store_x1(t, j):
                    wait_alone(sp, d.x1_ready, t + 1)
                    sp.dma_start(tile_rows(x1_dram, t, rows_of(t)), xin[j][0:rows_of(t), :])\
                        .then_inc(d.x1_stored[j], 16)
                tiles_in_turn(load_x, store_x1)

                sp.wait_ge(d.hid_ready, TILES)
                for j in range(2):
                    sp.wait_ge(d.x1_stored[j], 16 * (BODIES + 1 - j))

                def load_x1(t, j, uses):
                    if not isinstance(uses, int) or uses:
                        wait_alone(sp, fin_stored[j], uses * 16)
                    sp.dma_start(xin[j][0:rows_of(t), :], tile_rows(x1_dram, t, rows_of(t)))\
                        .then_inc(fin_loaded[j], 16)

                def store_out(t, j):
                    wait_alone(sp, fin_ready, t + 1)
                    sp.dma_start(tile_rows(out, t, rows_of(t)), xin[j][0:rows_of(t), :]).then_inc(fin_stored[j], 16)
                tiles_in_turn(load_x1, store_out)
                for j in range(2):
                    sp.wait_ge(fin_stored[j], 16 * (BODIES + 1 - j))

            def general():
                load = load_tiles(dense[1], x)

                load(0, 0, P)
                load(1, 1, P)

                def step(t, j):
                    load(t + 2, (j + 2) % 4, P)
                    store_x1(t, j, P)
                for t in range(4):
                    step(t, t)
                with sp.Fori(1, TILES // 4 - 1) as it:
                    for j in range(4):
                        step(it * 4 + j, j)
                for t in range(TILES - 5, TILES - 3):
                    step(t, t % 4)
                load(TILES - 1, 0, LAST)
                for t in range(TILES - 3, TILES - 1):
                    store_x1(t, t % 4, P)
                store_x1(TILES - 1, 0, LAST)

                sp.wait_ge(dense[1].hid_ready, TILES)
                for j in range(4):
                    sp.wait_ge(dense[1].x1_stored[j], 16 * ((TILES - 1 - j) // 4 + 1))

                def load_x1(t, j, n):
                    if not isinstance(t, int) or t >= 4:
                        wait_alone(sp, fin_stored[j], (t - j) * 4)
                    sp.dma_start(xin[j][0:n, :], tile_rows(x1_dram, t, n)).then_inc(fin_loaded[j], 16)
                tiles_of(load_x1)(sp)

            two_forms(sp, spread, general)

        @block.gpsimd
        def _(pool):
            g = nc.gpsimd
            for buf, value in ((before, 1.0), (pick, 0.0), (col_before, 1.0), (ones16, 1.0), (ones32, 1.0),
                               (col_count, 0.0), (tile_before, 1.0), (tile_after_neg, -1.0),
                               (tile_chunks, float(CHUNK_UNITS)), (tile_same, 0.0), (ident, 0.0), (zeros, 0.0),
                               (eps, EPS)):
                g.memset(buf[:], value).then_inc(filled, 1)
            g.iota(unit_id[:], pattern=[[P, UCOLS]], base=0, channel_multiplier=1,
                   allow_small_or_imprecise_dtypes=True).then_inc(filled, 1)
            g.iota(iota[:], pattern=[[1, P]], base=0, channel_multiplier=0,
                   allow_small_or_imprecise_dtypes=True).then_inc(constants, 1)
            g.iota(chunk_id[:], pattern=[[1, TCHUNKS // P]], base=0, channel_multiplier=TCHUNKS // P,
                   allow_small_or_imprecise_dtypes=True).then_inc(constants, 1)
            g.iota(spill[:], pattern=[[BLOCK_UNITS, BLOCKS]], base=SPILL, channel_multiplier=0,
                   allow_small_or_imprecise_dtypes=True).then_inc(constants, 1)
            g.iota(chunk_limit[:], pattern=[[SPAN, TILES]], base=SPAN + USE_AT + 1, channel_multiplier=0,
                   allow_small_or_imprecise_dtypes=True).then_inc(constants, 1)
            pool.wait_ge(filled, FILLS)
            for buf in (before, tile_before, tile_after_neg, tile_chunks, col_before):
                g.affine_select(out=buf[:], in_=buf[:], compare_op=ALU.is_ge, fill=0.0, base=-1,
                                pattern=[[1, buf.shape[1]]], channel_multiplier=-1).then_inc(constants, 1)
            for buf in (tile_same, ident):
                g.affine_select(out=buf[:], in_=buf[:], compare_op=ALU.not_equal, fill=1.0, base=0,
                                pattern=[[1, buf.shape[1]]], channel_multiplier=-1).then_inc(constants, 1)
            g.affine_select(out=pick[:], in_=pick[:], compare_op=ALU.not_equal, fill=1.0, base=-(P - 1),
                            pattern=[[1, 2 * P - 1]], channel_multiplier=0).then_inc(constants, 1)
            pool.wait_ge(constants, 12)
            g.memset(col_before[64:65, :], float(UNIT)).then_inc(constants, 1)
            g.memset(chunk_limit[:, TILES - 1:TILES], float(SPREAD_CHUNKS)).then_inc(constants, 1)
            g.memset(chunk_limit[:, TILES - 2:TILES - 1], float(SPREAD_CHUNKS - H)).then_inc(constants, 1)
            g.memset(tile_after_neg[:, TILES:TW], 0.0).then_inc(constants, 1)
            g.memset(tile_chunks[:, TILES:TW], 0.0).then_inc(constants, 1)
            pool.wait_ge(constants, CONSTANTS)

            def scatter(b, h):
                wait_alone(pool, units_out, b * 2 + 2)
                for u in range(UCOLS):
                    g.indirect_dma_start(
                        table, bass.IndirectOffsetOnAxis(ap=dest_now[h][:, u:u + 1], axis=0),
                        unit_out[h][:, u * UNIT:(u + 1) * UNIT, :].rearrange("p r v -> p (r v)"), None)\
                        .then_inc(scattered[h], 16)

            def zero_onehot(b):
                wait_alone(pool, ranked_done, b * GROUPS + GROUPS)
                g.tensor_copy(acc[:, bass.ds(b * ZW, ZW)].rearrange("p (z w) -> p z w", z=ZR), zeros_wide)\
                    .then_inc(onehot_zeroed, 1)

            pool.wait_ge(table_zeroed, 48)
            g.memset(acc[:, BLOCKS * ZW:TILES * D], 0.0).then_inc(onehot_zeroed, 1)
            with pool.Fori(0, BLOCKS // 2) as it:
                for h in range(2):
                    zero_onehot(it * 2 + h)
                    scatter(it * 2 + h, h)
            scatter(BLOCKS - 1, 0)
            zero_onehot(BLOCKS - 1)

            def gather_loop(ly, chunks):
                def gather(j):
                    g.indirect_dma_start(rows[j][:], None, support[ly.n],
                                         bass.IndirectOffsetOnAxis(ap=staged_index[:, j:j + 1], axis=0))\
                        .then_inc(ly.gathered[j], 16)
                for j in range(2):
                    pool.wait_ge(dense[ly.n].sup_stored[j], 16 * ((TILES - j + 1) // 2))
                for h in range(PARTS):
                    pool.wait_ge(ly.index_staged, h + 1)
                    if ly is layer[0] and h == 2:
                        pool.wait_ge(rows_turned, 4)
                    for j in range(h * H, h * H + H):
                        gather(j)
                def part(it, h):
                    wait_alone(pool, ly.index_staged, it * PARTS + (h + 1))
                    for j in range(h * H, h * H + H):
                        gather(j)
                with pool.Fori(1, chunks // U) as it:
                    for h in range(PARTS):
                        part(it, h)
                for h in range(chunks % U // H):
                    part(chunks // U, h)

            def zero_acc(t, j, n):
                wait_alone(pool, dense[1].x1_ready, t + 1)
                g.tensor_copy(tile_acc(t, P).rearrange("p (z w) -> p z w", z=KB), bcast(zeros[:, 0:P], 1, KB))\
                    .then_inc(acc_zeroed, 1)

            def spread():
                gather_loop(layer[0], SPREAD_CHUNKS)
                gather_loop(layer[1], SPREAD_CHUNKS)

            def general():
                gather_loop(layer[0], CHUNKS)
                tiles_of(zero_acc)(pool)
                gather_loop(layer[1], CHUNKS)

            two_forms(pool, spread, general)

        @block.tensor
        def _(pe):
            mm = nc.tensor.matmul
            pe.wait_ge(constants, CONSTANTS)

            def turn_tile(d, t, j, n):
                pe.wait_ge(d.hid_ready, t + 1)
                if not isinstance(t, int) or t >= 2:
                    pe.wait_ge(d.hidt_ready, t - 1)
                for q in range(KB):
                    last = nc.tensor.transpose(bank[j % 2][:, q * P:q * P + n], hid[j % 2][0:n, q * P:(q + 1) * P],
                                               ident[0:n, 0:n])
                last.then_inc(d.turned, 1)

            def product_part(d, t, j, n, q):
                if q == 0:
                    pe.wait_ge(d.hidt_ready, t + 1)
                    if not isinstance(t, int) or t >= 2:
                        pe.wait_ge(d.sup_ready, t - 1)
                part = mm(bank[2 + j % 2][0:n, :], hidt[j % 2][:, q * P:q * P + n], wt[d.n][:, q, :],
                          start=(q == 0), stop=(q == KB - 1))
                if q == KB - 1:
                    part.then_inc(d.product, 1)

            def product(d, t, j, n):
                for q in range(KB):
                    product_part(d, t, j, n, q)

            def slot(t, j2):
                if not isinstance(t, int) or t < TILES:
                    turn_tile(dense[0], t, j2, rows_of(t))
                if not isinstance(t, int) or t >= 1:
                    product(dense[0], t - 1, 1 - j2, rows_of(t - 1))

            pe.wait_ge(weights_loaded, 16 * (KB + 1))
            for kb in range(KB):
                if kb >= 1:
                    pe.wait_ge(w0_copied, kb)
                for q in range(KB):
                    nc.tensor.transpose(bank[5][:, q * P:(q + 1) * P], wload[q][:, kb * P:(kb + 1) * P],
                                        ident[:]).then_inc(w0t_ready, 1)

            def count_block(b, first=False, last=False):
                pe.wait_ge(onehot_ready, b + 1)
                for gr in range(GROUPS):
                    end = last and gr == GROUPS - 1
                    count = mm(bank[4][:, 0:GC * TILES], pick[:, bass.ds(P - 1 - gr - b * GROUPS, P)],
                               onehot[:, bass.ds(b * OH + gr * GC * TILES, GC * TILES)],
                               start=(first and gr == 0), stop=end)
                    if end:
                        count.then_inc(counted, 1)
            count_block(0, first=True)
            for b in range(1, BLOCKS):
                count_block(b, last=(b == BLOCKS - 1))
                t = b // 2 - 2
                if b % 2 == 0 and 0 <= t < COUNTING:
                    slot(t, t % 2)
            for t in range(COUNTING, COUNTING + 2):
                slot(t, t % 2)

            pe.wait_ge(col_count_in, 16)
            for b in range(BLOCKS):
                mm(bank[7][0:TILES, b:b + 1], col_count[:, b, 0:TILES], ones16[:], start=True, stop=True)\
                    .then_inc(tile_counts, 1)
            halves = ((0, 10), (10, BLOCKS))
            ones = ones32[:].to_broadcast([TILES, P])
            ones_half = ones16[0:TILES, :].to_broadcast([TILES, P])
            pe.wait_ge(start_terms, 1)
            pe.wait_ge(w0_copied, KB)
            for part, (lo, hi) in enumerate(halves):
                mm(bank[4 + part][:, 0:(hi - lo) * TW], ones_half, start_term[:, lo:hi, :].rearrange("p b t -> p (b t)"),
                   start=True, stop=True).then_inc(starts_ready, 1)
            pe.wait_ge(start_terms, 3)
            for part, (lo, hi) in enumerate(halves):
                at = bank[6 + part][:, 0:(hi - lo) * TW]
                mm(at, ones_half, after_term[:, lo:hi, :].rearrange("p b t -> p (b t)"), start=True, stop=False)
                mm(at, ones, before_term[:, lo:hi, :].rearrange("p b t -> p (b t)"), start=False, stop=False)
                pe.wait_ge(unit_steps, 7)
                mm(at.rearrange("p (b t) -> p b t", t=TW), chunks_f[:].to_broadcast([TILES, P]),
                   bcast(tile_chunks[:], 1, hi - lo), start=False, stop=True).then_inc(starts_ready, 1)
            mm(bank[7][:, CHUNK_STARTS:CHUNK_STARTS + TILES], chunks_f[:].to_broadcast([TILES, P]), tile_before[:, 1:TW],
               start=True, stop=True).then_inc(starts_ready, 1)
            for t in range(COUNTING + 2, EARLY):
                slot(t, t % 2)
            pe.wait_ge(starts_copied, 6)
            pe.wait_ge(col_start_ready, 2)
            pe.wait_ge(dest_steps, 6)

            def dense_phase(d):
                turn_tile(d, 0, 0, P)

                def step(t, j):
                    turn_tile(d, t + 1, (j + 1) % 4, P)
                    product(d, t, j, P)
                for t in range(4):
                    step(t, t)
                with pe.Fori(1, TILES // 4 - 1) as it:
                    for j in range(4):
                        step(it * 4 + j, j)
                for t in range(TILES - 5, TILES - 2):
                    step(t, t % 4)
                turn_tile(d, TILES - 1, 0, LAST)
                product(d, TILES - 2, 3, P)
                product(d, TILES - 1, 0, LAST)

            def rank(b, h, gr):
                no = (GROUPS * h + gr) % 2
                group = b * GROUPS + gr
                if not isinstance(b, int) or group >= 2:
                    pe.wait_ge(ranked_done, group - 1)
                at = bank[4 + no]
                mm(at[0:EP, 0:GC * TILES], before[:], onehot[:, bass.ds(group * GC * TILES, GC * TILES)],
                   start=True, stop=False)
                for i in range(GC):
                    k = gr * GC + i
                    last = mm(at[0:EP, i * TILES:(i + 1) * TILES], col_before[:, k:k + 1].to_broadcast([P, EP]),
                              col_count[:, bass.ds(b, 1), 0:TILES].rearrange("p a t -> p (a t)"),
                              start=False, stop=(i == GC - 1))
                last.then_inc(rank_ready, 1)

            def permute(b, h, gr):
                if gr == 0 and (not isinstance(b, int) or b >= 2):
                    pe.wait_ge(units_out, b * 2 - 2)
                no = (GROUPS * h + gr) % 2
                pe.wait_ge(perm_ready, b * GROUPS + (gr + 1))
                pe.wait_ge(perm_weighted, b * GROUPS + (gr + 1))
                for i in range(GC):
                    last = mm(bank[6 + h][:, 0:REC * COLS], perm_row[no][:, i, :],
                              perm_val[no][:, i, :, :].rearrange("p v c -> p (v c)"),
                              start=(gr == 0 and i == 0), stop=(gr == GROUPS - 1 and i == GC - 1))
                last.then_inc(permuted, 1)

            def sort_step(b, h, first=False, last=False):
                for gr in range(GROUPS):
                    if gr < GROUPS - 2 and not last:
                        rank(b, h, gr + 2)
                    if gr >= GROUPS - 2 and not last and not (isinstance(b, int) and b == BLOCKS - 1):
                        rank(b + 1, 1 - h, gr + 2 - GROUPS)
                    for i in range(BT):
                        if SLOT_GROUP[i] == gr and not last:
                            slot(b * BT + (EARLY + i), i)
                    if not first:
                        permute(b - 1, 1 - h, gr)

            rank(0, 0, 0)
            rank(0, 0, 1)
            sort_step(0, 0, first=True)
            sort_step(1, 1)
            with pe.Fori(1, BLOCKS // 2 - 1) as it:
                sort_step(it * 2, 0)
                sort_step(it * 2 + 1, 1)
            sort_step(BLOCKS - 3, 0)
            sort_step(BLOCKS - 2, 1)
            sort_step(BLOCKS - 1, 0)
            sort_step(BLOCKS, 1, last=True)

            for half in range(TCHUNKS // P // 4):
                pe.wait_ge(rows_loaded[half], 16 * 4)
                for v in range(REC):
                    for i in range(4):
                        rec = chunk_rows[4 * half + i].rearrange("c (m v) -> c v m", v=REC)[:, v, :]
                        last = nc.tensor.transpose(bank[2 * half + v][:, i * P:(i + 1) * P], rec, ident[:])
                    last.then_inc(rows_turned, 1)

            def chunk(ly, c, j, uses):
                pe.wait_ge(ly.sel_ready, c + 1)
                pe.wait_ge(ly.gathered[j], uses * 16 + 16)
                if not isinstance(c, int) or c >= 4:
                    pe.wait_ge(ly.added, c - 3)
                mm(bank[4 + j % 4][:], sel[:, j, :], rows[j][:], start=True, stop=True).then_inc(ly.summed, 1)

            def spread():
                def layer_spread(ly, d):
                    def body(it):
                        for k in range(2):
                            t = it * 2 + (k - 2)
                            dense_too = d is not None and (not isinstance(it, int) or t >= 0)
                            if dense_too:
                                turn_tile(d, t, k, P)
                            for i in range(SPAN):
                                at = k * SPAN + i
                                chunk(ly, it * BODY + at, at % U, it * (BODY // U) + at // U)
                                if dense_too and i in PART_AT:
                                    product_part(d, t, k, P, PART_AT.index(i))
                    spans(pe, body)
                    if d is not None:
                        turn_tile(d, TILES - 3, 0, P)
                    for j in range(TAIL):
                        chunk(ly, BODIES * BODY + j, j, BODIES * (BODY // U))
                        if d is not None and j in TAIL_PART_AT:
                            product_part(d, TILES - 3, 0, P, TAIL_PART_AT.index(j))
                    if d is not None:
                        turn_tile(d, TILES - 2, 1, P)
                        for q in range(KB):
                            product_part(d, TILES - 2, 1, P, q)
                            if q == 1:
                                turn_tile(d, TILES - 1, 0, LAST)
                        product(d, TILES - 1, 0, LAST)
                layer_spread(layer[0], dense[1])
                layer_spread(layer[1], None)

            def general():
                def layer_loop(ly):
                    for j in range(U):
                        chunk(ly, j, j, 0)
                    with pe.Fori(1, PASSES) as it:
                        for j in range(U):
                            chunk(ly, it * U + j, j, it)
                layer_loop(layer[0])
                dense_phase(dense[1])
                layer_loop(layer[1])

            two_forms(pe, spread, general)

        @block.vector
        def _(dve):
            v = nc.vector
            dve.wait_ge(edges_loaded, 48)
            v.tensor_scalar(edge_loc[:], edge_src[:], P - 1, None, ALU.bitwise_and).then_inc(prep, 1)
            dve.wait_ge(prep, 1)
            v.scalar_tensor_tensor(out=edge_dst[:], in0=edge_dst[:], scalar=7, in1=edge_loc[:],
                                   op0=ALU.logical_shift_left, op1=ALU.bitwise_or).then_inc(prep, 1)
            dve.wait_ge(prep, 2)
            v.tensor_scalar(edge_loc[:], edge_src[:], 7, None, ALU.logical_shift_right).then_inc(prep, 1)
            dve.wait_ge(prep, 3)
            v.tensor_copy(edge_tile, edge_loc[:]).then_inc(prep, 1)
            v.tensor_copy(edge_pack, edge_dst[:]).then_inc(prep, 1)
            dve.wait_ge(prep, 5)
            dve.wait_ge(constants, CONSTANTS)

            def statistics(d, t, j, n, use):
                dve.wait_ge(d.x_loaded[j], use * 16 + 16)
                if d.n == 1:
                    v.tensor_tensor(xin[j][0:n, :], xin[j][0:n, :], tile_acc(t, n), ALU.add)\
                        .then_inc(d.x1_ready, 1)
                    dve.wait_ge(d.x1_ready, t + 1)
                v.bn_stats(stats[0:n, j, :], xin[j][0:n, :]).then_inc(d.stats_done, 1)
                wait_alone(dve, d.stats_done, t + 1)
                v.bn_aggr(mv[0:n, j, :], stats[0:n, j, :]).then_inc(d.mv_ready, 1)

            def scales(d, t, j, n):
                dve.wait_ge(d.std_ready, t + 1)
                v.reciprocal(rstd[0:n, j, :], std[0:n, j, :]).then_inc(d.rstd_ready, 1)
                dve.wait_ge(d.rstd_ready, t + 1)
                v.tensor_scalar(nmr[0:n, j, :], mv[0:n, j, 0:1], rstd[0:n, j, :], -1.0, ALU.mult, ALU.mult)\
                    .then_inc(d.norm_ready, 1)

            def copy_turned(d, t, j, n):
                dve.wait_ge(d.turned, t + 1)
                if not isinstance(t, int) or t >= 2:
                    dve.wait_ge(d.product, t - 1)
                v.tensor_copy(hidt[j % 2][:].rearrange("p (q m) -> p q m", q=KB)[:, :, 0:n],
                              bank[j % 2][:].rearrange("p (q m) -> p q m", q=KB)[:, :, 0:n])\
                    .then_inc(d.hidt_ready, 1)

            def slot(t, i, uses):
                some = not isinstance(t, int)
                if some or t + 1 < TILES:
                    scales(dense[0], t + 1, (i + 1) % 4, rows_of(t + 1))
                if some or t + 2 < TILES:
                    statistics(dense[0], t + 2, (i + 2) % 4, rows_of(t + 2), uses + (i + 2) // 4)

            def onehots(b):
                v.tensor_tensor(onehot[:, b * OH:(b + 1) * OH].rearrange("p (k t) -> p k t", k=BC),
                                bcast(edge_tile[:, b * BC:(b + 1) * BC], 2, TILES),
                                bcast(iota[0:EP, 0:TILES], 1, BC), ALU.is_equal).then_inc(onehot_ready, 1)

            onehots(0)
            statistics(dense[0], 0, 0, P, 0)
            statistics(dense[0], 1, 1, P, 0)
            for b in range(1, BLOCKS):
                onehots(b)
                t = b // 2 - 2
                if b == 3:
                    scales(dense[0], 0, 0, P)
                if b % 2 == 0 and 0 <= t < COUNTING:
                    slot(t, t % 4, t // 4)
            for t in range(COUNTING, COUNTING + 2):
                slot(t, t % 4, t // 4)

            dve.wait_ge(tile_counts, BLOCKS)
            steps = iter(range(1, 100))

            def counted_step(ins):
                n = next(steps)
                ins.then_inc(unit_steps, 1)
                dve.wait_ge(unit_steps, n)
            counted_step(v.tensor_scalar(units_i[:], bank[7][0:TILES, 0:BLOCKS], float(UNIT - 1), None, ALU.add))
            counted_step(v.tensor_scalar(units_i[:], units_i[:], UNIT_LOG, None, ALU.logical_shift_right))
            counted_step(v.tensor_copy(units_f[:], units_i[:]))

            def term(out, per_block, per_tile):
                v.tensor_tensor(out, bcast(per_block[:], 2, TW), bcast(per_tile[:], 1, BLOCKS), ALU.mult)\
                    .then_inc(start_terms, 1)
            term(start_term, units_f, tile_before)
            counted_step(v.tensor_tensor_scan(units_to[:], units_f[:], zeros[0:TILES, 0:BLOCKS], 0.0,
                                              ALU.add, ALU.add))
            v.tensor_scalar(chunks_i[:], units_to[:, BLOCKS - 1:BLOCKS], float(CHUNK_UNITS - 1), None, ALU.add)\
                .then_inc(unit_steps, 1)
            next(steps)
            counted_step(v.tensor_tensor(units_before[:], units_to[:], units_f[:], ALU.subtract))
            term(before_term, units_before, tile_same)
            term(after_term, units_f, tile_after_neg)
            v.tensor_scalar(chunks_i[:], chunks_i[:], CHUNK_UNITS_LOG, None, ALU.logical_shift_right).then_inc(prep, 1)
            dve.wait_ge(prep, 6)
            counted_step(v.tensor_copy(chunks_f[:], chunks_i[:]))

            slot(COUNTING + 2, (COUNTING + 2) % 4, (COUNTING + 2) // 4)
            dve.wait_ge(starts_copied, 6)

            def dest_step(n, ins):
                ins.then_inc(dest_steps, 1)
                dve.wait_ge(dest_steps, n)
            uid = bcast(unit_id[:], 1, BLOCKS)
            dest_step(1, v.tensor_tensor(shift_step[:], unit_shift[:, :, 1:TW], unit_shift[:, :, 0:TILES],
                                         ALU.subtract))
            for first in range(0, UCOLS, MASKS):
                some = range(first, min(first + MASKS, UCOLS))
                if first:
                    dve.wait_ge(unit_dest_done, first)
                for u in some:
                    v.scalar_tensor_tensor(out=unit_mask[u - first], in0=unit_start[:, :, 1:TW],
                                           scalar=unit_id[:, u:u + 1], in1=shift_step[:],
                                           op0=ALU.is_le, op1=ALU.mult).then_inc(unit_masked, 1)
                for u in some:
                    dve.wait_ge(unit_masked, u + 1)
                    v.tensor_reduce(unit_dest[:, :, u], unit_mask[u - first], AX.X, ALU.add)\
                        .then_inc(unit_dest_done, 1)
                    t = COUNTING + 3 + u // 2
                    if u % 2 == 0 and t < EARLY:
                        slot(t, t % 4, t // 4)
            dve.wait_ge(unit_dest_done, UCOLS)
            dest_step(2, v.tensor_tensor(unit_dest[:], unit_dest[:], uid, ALU.add))
            v.tensor_tensor(unit_dest_i[:].rearrange("p (b u) -> p b u", b=BLOCKS), unit_dest[:],
                            bcast(unit_shift[:, :, 0], 2, UCOLS), ALU.add).then_inc(dest_steps, 1)
            dest_step(4, v.tensor_tensor(chunk_mask[:], bcast(chunk_id[:], 2, TILES),
                                         bcast(chunk_start[:], 1, TCHUNKS // P), ALU.is_ge))
            dest_step(5, v.tensor_reduce(chunk_tile_f[:], chunk_mask[:, :, 0:TILES - 1], AX.X, ALU.add))
            dest_step(6, v.tensor_scalar(chunk_tile_i[:], chunk_tile_f[:], float(D), None, ALU.mult))
            v.tensor_tensor(tile_late[:], chunk_start[0:1, :], chunk_limit[:], ALU.is_gt).then_inc(late_steps, 1)
            dve.wait_ge(late_steps, 1)
            v.tensor_reduce(late_f[:], tile_late[:], AX.X, ALU.add).then_inc(late_steps, 1)
            dve.wait_ge(late_steps, 2)
            v.tensor_copy(late_i[:], late_f[:]).then_inc(late_steps, 1)

            def dense_phase(d):
                def norm(t, j, n, use):
                    statistics(d, t, j, n, use)
                    scales(d, t, j, n)

                def step(t, j, it):
                    norm(t + 1, (j + 1) % 4, P, it + (j + 1) // 4)
                    copy_turned(d, t, j, P)

                norm(0, 0, P, 0)
                for t in range(4):
                    step(t, t, 0)
                with dve.Fori(1, TILES // 4 - 1) as it:
                    for j in range(4):
                        step(it * 4 + j, j, it)
                for t in range(TILES - 5, TILES - 2):
                    step(t, t % 4, t // 4)
                norm(TILES - 1, 0, LAST, (TILES - 1) // 4)
                copy_turned(d, TILES - 2, 3, P)
                copy_turned(d, TILES - 1, 0, LAST)

            def rank(b, h, gr):
                no = (GROUPS * h + gr) % 2
                group = b * GROUPS + gr
                dve.wait_ge(rank_ready, group + 1)
                v.tensor_tensor(ranked[no][:], bank[4 + no][0:EP, 0:GC * TILES].rearrange("p (k t) -> p k t", k=GC),
                                onehot[:, bass.ds(group * GC * TILES, GC * TILES)]
                                .rearrange("p (k t) -> p k t", k=GC), ALU.mult).then_inc(ranked_done, 1)
                dve.wait_ge(ranked_done, group + 1)
                v.tensor_reduce(place[:, gr * GC:(gr + 1) * GC], ranked[no][:], AX.X, ALU.add).then_inc(placed, 1)

            def places(b, h):
                dve.wait_ge(placed, b * GROUPS + GROUPS)
                v.tensor_copy(place_i[:], place[:]).then_inc(place_steps, 1)
                dve.wait_ge(place_steps, b * 5 + 1)
                v.tensor_scalar(prow_i[:], place_i[:], UNIT_LOG, P - 1, ALU.logical_shift_right, ALU.bitwise_and)\
                    .then_inc(place_steps, 1)
                v.tensor_scalar(pcol_i[:], place_i[:], 7 + UNIT_LOG, UNIT_LOG, ALU.logical_shift_right,
                                ALU.logical_shift_left).then_inc(place_steps, 1)
                dve.wait_ge(place_steps, b * 5 + 3)
                v.scalar_tensor_tensor(out=pcol_i[:], in0=place_i[:], scalar=UNIT - 1, in1=pcol_i[:],
                                       op0=ALU.bitwise_and, op1=ALU.bitwise_or).then_inc(place_steps, 1)
                v.tensor_copy(prow[h][:], prow_i[:]).then_inc(place_steps, 1)
                dve.wait_ge(place_steps, b * 5 + 5)
                v.tensor_copy(pcol[h][:], pcol_i[:]).then_inc(prep, 1)
                dve.wait_ge(prep, b + 7)

            def operands(b, h, gr):
                no = (GROUPS * h + gr) % 2
                group = b * GROUPS + gr
                c = bass.ds(group * GC, GC)
                if not isinstance(b, int) or group >= 2:
                    dve.wait_ge(permuted, group - 1)
                v.tensor_tensor(perm_col[no], bcast(iota[0:EP, 0:COLS], 1, GC),
                                bcast(pcol[h][:, gr * GC:(gr + 1) * GC], 2, COLS), ALU.is_equal)\
                    .then_inc(perm_steps, 1)
                v.tensor_tensor(perm_row[no], bcast(iota[0:EP, :], 1, GC),
                                bcast(prow[h][:, gr * GC:(gr + 1) * GC], 2, P), ALU.is_equal)
                dve.wait_ge(perm_steps, group + 1)
                v.tensor_tensor(perm_val[no][:, :, 0, :], perm_col[no], bcast(edge_pack[:, c], 2, COLS), ALU.mult)\
                    .then_inc(perm_ready, 1)

            def sort_step(b, h, pair, first=False, last=False):
                for gr in range(GROUPS):
                    for i in range(BT):
                        if SLOT_GROUP[i] == gr and not last:
                            slot(b * BT + (EARLY + i), 2 * h + i, pair + EARLY // 4)
                    if not last:
                        rank(b, h, gr)
                    if not first:
                        operands(b - 1, 1 - h, gr)
                if not last:
                    places(b, h)

            sort_step(0, 0, 0, first=True)
            sort_step(1, 1, 0)
            with dve.Fori(1, BLOCKS // 2 - 1) as it:
                sort_step(it * 2, 0, it)
                sort_step(it * 2 + 1, 1, it)
            sort_step(BLOCKS - 3, 0, BLOCKS // 2 - 1)
            sort_step(BLOCKS - 2, 1, BLOCKS // 2 - 1)
            sort_step(BLOCKS - 1, 0, BLOCKS // 2)
            sort_step(BLOCKS, 1, BLOCKS // 2, last=True)

            for half in range(TCHUNKS // P // 4):
                s = slice(half * D, (half + 1) * D)
                dve.wait_ge(rows_turned, 2 * half + 1)
                v.tensor_copy(pack_i, bank[2 * half][:]).then_inc(table_steps, 1)
                dve.wait_ge(table_steps, 2 * half + 1)
                v.tensor_scalar(row_index[:, s], pack_i, 7, None, ALU.logical_shift_right).then_inc(table_ready[half], 1)
                v.tensor_scalar(loc_i, pack_i, P - 1, None, ALU.bitwise_and).then_inc(table_steps, 1)
                dve.wait_ge(table_steps, 2 * half + 2)
                v.tensor_copy(local_row[:, s], loc_i).then_inc(table_ready[half], 1)
            for half in range(2):
                dve.wait_ge(table_ready[half], 3)
            dve.wait_ge(onehot_zeroed, BLOCKS + 1)
            dve.wait_ge(chunk_tile_in, 16)

            def select(ly, c, j):
                if not isinstance(c, int) or c >= U:
                    dve.wait_ge(ly.summed, c - (U - 1))
                v.tensor_scalar(sel[:, j, :], iota[:], local_row[:, bass.ds(c, 1)], weight[:, bass.ds(c, 1)],
                                ALU.is_equal, ALU.mult).then_inc(ly.sel_ready, 1)

            def add(ly, c, j, where):
                dve.wait_ge(ly.summed, c + 1)
                if not isinstance(c, int) or c >= 1:
                    dve.wait_ge(ly.added, c)
                at = acc[:, bass.ds(where, D)]
                v.tensor_tensor(at, bank[4 + j % 4][:], at, ALU.add).then_inc(ly.added, 1)

            def places_of(first):
                _, where = nc.values_load_multi_w_load_instructions(
                    chunk_tile[0:1, bass.ds(first, U)], engines=[DVE], min_val=0, max_val=(TILES - 1) * D,
                    skip_runtime_bounds_check_because="a count of at most TILES - 1 comparisons, times D")
                return where

            def finish(t, j, n, uses):
                dve.wait_ge(fin_loaded[j], uses * 16 + 16)
                v.scalar_tensor_tensor(out=xin[j][0:n, :], in0=tile_acc(t, n), scalar=0.0, in1=xin[j][0:n, :],
                                       op0=ALU.max, op1=ALU.add).then_inc(fin_ready, 1)

            def spread():
                def layer_spread(ly, use, use_more):
                    def body(it):
                        for at in range(BODY):
                            k, i = at // SPAN, at % SPAN
                            if at % U == 0:
                                where = places_of(it * BODY + at)
                            add(ly, it * BODY + at, at % U, where[at % U])
                            select(ly, it * BODY + (at + U), at % U)
                            t = it * 2 + (k - 1)
                            if isinstance(it, int) and t < 0:
                                continue
                            if i == USE_AT:
                                dve.wait_ge(ly.added, it * BODY + (at + 1))
                                use(t, 1 - k, it + (k - 1))
                            if i == USE_AT + 2:
                                use_more(t, 1 - k)
                    for j in range(U):
                        select(ly, j, j)
                    spans(dve, body)
                    where = places_of(BODIES * BODY)
                    for j in range(TAIL):
                        add(ly, BODIES * BODY + j, j, where[j])
                        if j == TAIL - H - 1:
                            dve.wait_ge(ly.added, SPREAD_CHUNKS - H)
                            use(TILES - 2, 1, BODIES - 1)
                        if j == TAIL - H + 1:
                            use_more(TILES - 2, 1)
                    dve.wait_ge(ly.added, SPREAD_CHUNKS)
                    use(TILES - 1, 0, BODIES)
                    use_more(TILES - 1, 0)

                d = dense[1]
                layer_spread(layer[0], lambda t, j, uses: statistics(d, t, j, rows_of(t), uses),
                             lambda t, j: scales(d, t, j, rows_of(t)))
                dve.wait_ge(acc_zeroed, TILES)
                layer_spread(layer[1], lambda t, j, uses: finish(t, j, rows_of(t), uses), lambda t, j: None)

            def general():
                def layer_loop(ly):
                    def one(it):
                        where = places_of(it * U)
                        for j in range(U):
                            add(ly, it * U + j, j, where[j])
                            select(ly, it * U + (U + j), j)
                    for j in range(U):
                        select(ly, j, j)
                    one(0)
                    with dve.Fori(1, PASSES - 1) as it:
                        one(it)
                    where = places_of((PASSES - 1) * U)
                    for j in range(U):
                        add(ly, (PASSES - 1) * U + j, j, where[j])
                    dve.wait_ge(ly.added, CHUNKS)

                layer_loop(layer[0])
                dense_phase(dense[1])
                dve.wait_ge(acc_zeroed, TILES)
                layer_loop(layer[1])
                for t in range(4):
                    finish(t, t, P, 0)
                with dve.Fori(1, TILES // 4) as it:
                    for j in range(4):
                        finish(it * 4 + j, j, P, it)
                finish(TILES - 1, 0, LAST, TILES // 4)

            two_forms(dve, spread, general)

        @block.scalar
        def _(act):
            a = nc.scalar
            act.wait_ge(constants, CONSTANTS)
            def root(d, t, j, n):
                act.wait_ge(d.mv_ready, t + 1)
                a.activation(std[0:n, j, :], mv[0:n, j, 1:2], ACT.Sqrt, bias=eps[0:n, :]).then_inc(d.std_ready, 1)

            def hidden(d, t, j, j2, n):
                act.wait_ge(d.norm_ready, t + 1)
                if not isinstance(t, int) or t >= 2:
                    act.wait_ge(d.turned, t - 1)
                a.activation(hid[j2][0:n, :], xin[j][0:n, :], ACT.Relu, bias=nmr[0:n, j, :],
                             scale=rstd[0:n, j, :]).then_inc(d.hid_ready, 1)

            def copy_turned(d, t, j2, n):
                act.wait_ge(d.turned, t + 1)
                if not isinstance(t, int) or t >= 2:
                    act.wait_ge(d.product, t - 1)
                a.copy(hidt[j2][:].rearrange("p (q m) -> p q m", q=KB)[:, :, 0:n],
                       bank[j2][:].rearrange("p (q m) -> p q m", q=KB)[:, :, 0:n]).then_inc(d.hidt_ready, 1)

            def store(d, t, j2, n):
                act.wait_ge(d.product, t + 1)
                if not isinstance(t, int):
                    act.wait_ge(d.sup_stored[j2], (t - j2) * 8)
                elif t >= 2:
                    act.wait_ge(d.sup_stored[j2], (t - j2) * 8)
                a.copy(sup[j2][0:n, :], bank[2 + j2][0:n, :]).then_inc(d.sup_ready, 1)
                act.wait_ge(d.sup_ready, t + 1)
                act.dma_start(tile_rows(support[d.n], t, n), sup[j2][0:n, :]).then_inc(d.sup_stored[j2], 16)

            def slot(t, i):
                d, some = dense[0], not isinstance(t, int)
                if some or t + 1 < TILES:
                    hidden(d, t + 1, (i + 1) % 4, (i + 1) % 2, rows_of(t + 1))
                if some or t + 2 < TILES:
                    root(d, t + 2, (i + 2) % 4, rows_of(t + 2))

            def slot_turned(t, i):
                if not isinstance(t, int) or t < TILES:
                    copy_turned(dense[0], t, i % 2, rows_of(t))

            def slot_store(t, i):
                if not isinstance(t, int) or t >= 1:
                    store(dense[0], t - 1, (i + 1) % 2, rows_of(t - 1))

            def early(t):
                slot(t, t % 4)
                slot_turned(t, t % 4)
                slot_store(t, t % 4)

            for kb in range(KB):
                act.wait_ge(w0t_ready, KB * (kb + 1))
                a.copy(wt[0][:, kb, :], bank[5][:]).then_inc(w0_copied, 1)
            root(dense[0], 0, 0, P)
            hidden(dense[0], 0, 0, 0, P)
            root(dense[0], 1, 1, P)
            for t in range(COUNTING):
                early(t)
            act.wait_ge(counted, 1)
            a.copy(group_count, bank[4][0:BLOCKS * GROUPS, 0:GC * TILES]).then_inc(group_count_ready, 1)
            for t in range(COUNTING, COUNTING + 2):
                early(t)
            halves = ((0, 10), (10, BLOCKS))
            act.wait_ge(tile_counts, BLOCKS)
            act.wait_ge(starts_ready, 2)
            for part, (lo, hi) in enumerate(halves):
                w = (hi - lo) * TW
                a.copy(unit_start[:, lo:hi, :].rearrange("p b t -> p (b t)"), bank[4 + part][:, 0:w])\
                    .then_inc(starts_copied, 1)
                a.copy(col_count[64:65, lo:hi, :].rearrange("p b t -> p (b t)"), bank[4 + part][64:65, 0:w])\
                    .then_inc(col_start_ready, 1)
            act.wait_ge(starts_ready, 5)
            for part, (lo, hi) in enumerate(halves):
                w = (hi - lo) * TW
                a.copy(unit_shift[:, lo:hi, 0:TILES],
                       bank[6 + part][:, 0:w].rearrange("p (b t) -> p b t", t=TW)[:, :, 0:TILES])\
                    .then_inc(starts_copied, 1)
            a.copy(unit_shift[:, :, TILES], spill[:]).then_inc(starts_copied, 1)
            a.copy(chunk_start[:], bank[7][:, CHUNK_STARTS:CHUNK_STARTS + TILES]).then_inc(starts_copied, 1)
            for t in range(COUNTING + 2, EARLY):
                early(t)

            def dense_phase(d):
                def norm(t, j, n):
                    root(d, t, j, n)
                    hidden(d, t, j, j % 2, n)

                norm(0, 0, P)
                norm(1, 1, P)

                def step(t, j):
                    norm(t + 2, (j + 2) % 4, P)
                    store(d, t, j % 2, P)
                for t in range(4):
                    step(t, t)
                with act.Fori(1, TILES // 4 - 1) as it:
                    for j in range(4):
                        step(it * 4 + j, j)
                for t in range(TILES - 5, TILES - 3):
                    step(t, t % 4)
                norm(TILES - 1, 0, LAST)
                for t in range(TILES - 3, TILES - 1):
                    store(d, t, t % 2, P)
                store(d, TILES - 1, 0, LAST)

            def units(b, h):
                act.wait_ge(permuted, b * GROUPS + GROUPS)
                if not isinstance(b, int):
                    act.wait_ge(scattered[h], (b - h) * (8 * UCOLS))
                elif b >= 2:
                    act.wait_ge(scattered[h], 16 * UCOLS * (b // 2))
                a.copy(unit_out[h][:], bank[6 + h][:, 0:REC * COLS]
                       .rearrange("p (v c) -> p c v", v=REC)).then_inc(units_out, 1)
                a.copy(dest_now[h][:], unit_dest_i[:, bass.ds(b * UCOLS, UCOLS)]).then_inc(units_out, 1)

            def weigh(b, h, gr):
                no = (GROUPS * h + gr) % 2
                group = b * GROUPS + gr
                act.wait_ge(perm_steps, group + 1)
                if not isinstance(b, int) or group >= 2:
                    act.wait_ge(permuted, group - 1)
                for i in range(GC):
                    last = a.activation(perm_val[no][:, i, 1, :], perm_col[no][:, i, :], ACT.Copy,
                                        scale=edge_w[:, bass.ds(group * GC + i, 1)])
                last.then_inc(perm_weighted, 1)

            def sort_step(b, h, first=False, last=False):
                for gr in range(GROUPS):
                    here = gr in SLOT_GROUP and not last
                    if here:
                        i = SLOT_GROUP.index(gr)
                        t, ring = b * BT + (EARLY + i), 2 * h + i
                        slot(t, ring)
                    if not first:
                        weigh(b - 1, 1 - h, gr)
                    if gr == 0 and not (isinstance(b, int) and b < 2):
                        units(b - 2, h)
                    if here:
                        slot_turned(t, ring)
                    if gr - 1 in SLOT_GROUP and not last:
                        slot_store(t, ring)
                if last:
                    units(BLOCKS - 1, 0)

            sort_step(0, 0, first=True)
            sort_step(1, 1)
            with act.Fori(1, BLOCKS // 2 - 1) as it:
                sort_step(it * 2, 0)
                sort_step(it * 2 + 1, 1)
            sort_step(BLOCKS - 3, 0)
            sort_step(BLOCKS - 2, 1)
            sort_step(BLOCKS - 1, 0)
            sort_step(BLOCKS, 1, last=True)

            def stage(ly, first, h):
                if not isinstance(first, int) or first >= U:
                    act.wait_ge(ly.summed, first + (H - U))
                a.copy(staged_index[:, h * H:(h + 1) * H], row_index[:, bass.ds(first, H)]).then_inc(ly.index_staged, 1)

            for half in range(TCHUNKS // P // 4):
                act.wait_ge(rows_turned, 2 * half + 2)
                a.copy(weight[:, half * D:(half + 1) * D], bank[2 * half + 1][:]).then_inc(table_ready[half], 1)
                act.wait_ge(table_ready[half], 3)
                if half == 0:
                    for h in range(PARTS):
                        stage(layer[0], h * H, h)

            def spread():
                d = dense[1]

                def zero_acc(t):
                    act.wait_ge(d.x1_ready, t + 1)
                    a.copy(tile_acc(t, P).rearrange("p (z w) -> p z w", z=KB), bcast(zeros[:, 0:P], 1, KB))\
                        .then_inc(acc_zeroed, 1)

                def layer_spread(ly, with_tiles):
                    def body(it):
                        for k in range(2):
                            t = it * 2 + (k - 1)
                            now = with_tiles and (not isinstance(it, int) or t >= 0)
                            before = with_tiles and (not isinstance(it, int) or t >= 1)
                            if before:
                                copy_turned(d, t - 1, k, P)
                            for m in range(6):
                                if m == 4 and now:
                                    root(d, t, 1 - k, P)
                                    zero_acc(t)
                                    hidden(d, t, 1 - k, 1 - k, P)
                                if m == 5 and before:
                                    store(d, t - 1, k, P)
                                stage(ly, it * BODY + (k * SPAN + U + m * H), (2 * k + m) % PARTS)
                    if ly is not layer[0]:
                        for h in range(PARTS):
                            stage(ly, h * H, h)
                    spans(act, body)
                    if with_tiles:
                        def normed(t):
                            root(d, t, t % 2, rows_of(t))
                            zero_acc(t)
                            hidden(d, t, t % 2, t % 2, rows_of(t))
                        copy_turned(d, TILES - 3, 0, P)
                        normed(TILES - 2)
                        store(d, TILES - 3, 0, P)
                        copy_turned(d, TILES - 2, 1, P)
                        normed(TILES - 1)
                        copy_turned(d, TILES - 1, 0, LAST)
                        store(d, TILES - 2, 1, P)
                        store(d, TILES - 1, 0, LAST)
                layer_spread(layer[0], True)
                layer_spread(layer[1], False)

            def general():
                def stage_indices(ly):
                    if ly is not layer[0]:
                        for h in range(PARTS):
                            stage(ly, h * H, h)
                    with act.Fori(1, PASSES) as it:
                        for h in range(PARTS):
                            stage(ly, it * U + h * H, h)

                stage_indices(layer[0])
                dense_phase(dense[1])
                stage_indices(layer[1])

                def store_out(t, j, n):
                    act.wait_ge(fin_ready, t + 1)
                    act.dma_start(tile_rows(out, t, n), xin[j][0:n, :]).then_inc(fin_stored[j], 16)
                tiles_of(store_out)(act)
                for j in range(4):
                    act.wait_ge(fin_stored[j], 16 * ((TILES - 1 - j) // 4 + 1))

            two_forms(act, spread, general)


def kernel(x, src, dst, edge_weight, L0_gnn_weight, L1_gnn_weight):
    import numpy as np
    import concourse.bacc as bacc
    from concourse.bass_utils import run_bass_kernel_spmd as run

    nc = bacc.Bacc("TRN2", target_bir_lowering=False, num_devices=1)
    arrays = {"x": x, "src": src, "dst": dst, "edge_weight": edge_weight, "w0": L0_gnn_weight, "w1": L1_gnn_weight}
    arrays = {f"in_{k}": np.ascontiguousarray(a) for k, a in arrays.items()}
    args = [nc.dram_tensor(k, a.shape, mybir.dt.from_np(a.dtype), kind="ExternalInput").ap()
            for k, a in arrays.items()]
    out = nc.dram_tensor("out_0", (NODES, D), F32, kind="ExternalOutput").ap()
    build_gnn(nc, *args, out)
    return run(nc, [arrays], core_ids=[0]).results[0]["out_0"]
```
